# Optimizing a Trainium2 kernel written in Bass

```python
import numpy as np
import jax
import jax.numpy as jnp

def _softmax(x, axis=-1):
    return jax.nn.softmax(x, axis=axis)

def _gelu(x):
    return jax.nn.gelu(x, approximate=True)

def _silu(x):
    return jax.nn.silu(x)

def _sigmoid(x):
    return jax.nn.sigmoid(x)

def _layernorm(x, axis=-1, eps=1e-05):
    m = jnp.mean(x, axis=axis, keepdims=True)
    v = jnp.var(x, axis=axis, keepdims=True)
    return (x - m) / jnp.sqrt(v + eps)

def _scatter_add(tgt, idx, src, axis=0):
    return tgt.at[idx].add(src)

def _segment_sum(src, seg, n):
    return jax.ops.segment_sum(src, seg, n)
kernel_name = 'mk_gnn_preln_d1_gnn_r8_a04aca'

def setup_inputs(seed: int=0):
    np.random.seed(seed)
    _w = jnp.asarray

    def _rec_inputs():
        import jax
        import jax.numpy as jnp
        _gk = jax.random.key(seed)
        x = -0.000202 + 1 * jax.random.normal(jax.random.fold_in(_gk, 1), (6250, 128), jnp.float32)
        src = jax.random.randint(jax.random.fold_in(_gk, 2), (100000,), 0, 6250, jnp.int32)
        dst = jax.random.randint(jax.random.fold_in(_gk, 3), (100000,), 0, 6250, jnp.int32)
        _o = jnp.argsort(dst, stable=True)
        src = src[_o]
        dst = dst[_o]
        edge_attr_128 = -8.16379e-05 + 0.999858 * jax.random.normal(jax.random.fold_in(_gk, 12), (100000, 128), jnp.float32)
        return (x, src, dst, edge_attr_128)
    x, src, dst, edge_attr_128 = _rec_inputs()

    def _L0_gnn_setup():
        import jax, jax.numpy as jnp
        import numpy as np
        N_NODES = 6250
        N_EDGES = 100000
        D_IN = 128
        OUT = 128
        H = 4
        D = OUT // H
        NEG_SLOPE = 0.2

        def _leaky_relu(x):
            return jnp.where(x >= 0, x, NEG_SLOPE * x)

        def _edge_softmax(e, dst, n_nodes):
            m = jax.ops.segment_max(e, dst, num_segments=n_nodes)
            m = jnp.where(jnp.isfinite(m), m, 0.0)
            ex = jnp.exp(e - m[dst])
            s = jax.ops.segment_sum(ex, dst, num_segments=n_nodes)
            return ex / s[dst]
        key = jax.random.key(seed)
        ks = jax.random.split(key, 10)
        return {'X': jax.random.normal(ks[0], (N_NODES, D_IN), dtype=jnp.float32), 'X_edge': jax.random.normal(ks[1], (N_EDGES, D_IN), dtype=jnp.float32), 'W_src': jax.random.normal(ks[2], (OUT, D_IN), dtype=jnp.float32) * 0.05, 'W_dst': jax.random.normal(ks[3], (OUT, D_IN), dtype=jnp.float32) * 0.05, 'W_edge': jax.random.normal(ks[4], (OUT, D_IN), dtype=jnp.float32) * 0.05, 'attn_src': jax.random.normal(ks[5], (H, D), dtype=jnp.float32), 'attn_dst': jax.random.normal(ks[6], (H, D), dtype=jnp.float32), 'attn_edge': jax.random.normal(ks[7], (H, D), dtype=jnp.float32), 'src': jax.random.randint(ks[8], (N_EDGES,), 0, N_NODES, dtype=jnp.int32), 'dst': jax.random.randint(ks[9], (N_EDGES,), 0, N_NODES, dtype=jnp.int32)}
    _L0_gnn_all = _L0_gnn_setup()
    _L0_gnn_in = {k: v for k, v in _L0_gnn_all.items() if k in ('W_src', 'W_dst', 'W_edge', 'attn_src', 'attn_dst', 'attn_edge')}
    del _L0_gnn_all
    return {'x': x, 'src': src, 'dst': dst, 'edge_attr_128': edge_attr_128, 'L0_gnn_W_src': _L0_gnn_in['W_src'], 'L0_gnn_W_dst': _L0_gnn_in['W_dst'], 'L0_gnn_W_edge': _L0_gnn_in['W_edge'], 'L0_gnn_attn_src': _L0_gnn_in['attn_src'], 'L0_gnn_attn_dst': _L0_gnn_in['attn_dst'], 'L0_gnn_attn_edge': _L0_gnn_in['attn_edge']}

def reference(x, src, dst, edge_attr_128, L0_gnn_W_src, L0_gnn_W_dst, L0_gnn_W_edge, L0_gnn_attn_src, L0_gnn_attn_dst, L0_gnn_attn_edge):
    import jax
    import jax.numpy as jnp

    def _L0_gnn_ref(X, X_edge, W_src, W_dst, W_edge, attn_src, attn_dst, attn_edge, src, dst):
        import jax, jax.numpy as jnp
        import numpy as np
        N_NODES = 6250
        N_EDGES = 100000
        D_IN = 128
        OUT = 128
        H = 4
        D = OUT // H
        NEG_SLOPE = 0.2

        def _leaky_relu(x):
            return jnp.where(x >= 0, x, NEG_SLOPE * x)

        def _edge_softmax(e, dst, n_nodes):
            m = jax.ops.segment_max(e, dst, num_segments=n_nodes)
            m = jnp.where(jnp.isfinite(m), m, 0.0)
            ex = jnp.exp(e - m[dst])
            s = jax.ops.segment_sum(ex, dst, num_segments=n_nodes)
            return ex / s[dst]
        n = X.shape[0]
        h_src = (X @ W_src.T).reshape(n, H, D)
        h_dst = (X @ W_dst.T).reshape(n, H, D)
        e_src = jnp.einsum('nhd,hd->nh', h_src, attn_src)
        e_dst = jnp.einsum('nhd,hd->nh', h_dst, attn_dst)
        e = _leaky_relu(e_src[src] + e_dst[dst])
        a = _edge_softmax(e, dst, n)
        m = a[:, :, None] * h_src[src]
        h_neigh = jax.ops.segment_sum(m, dst, num_segments=n)
        h_edge = (X_edge @ W_edge.T).reshape(-1, H, D)
        e_edge = jnp.einsum('ehd,hd->eh', h_edge, attn_edge)
        e2 = _leaky_relu(e_edge + e_dst[dst])
        a2 = _edge_softmax(e2, dst, n)
        h_edge_agg = jax.ops.segment_sum(a2[:, :, None] * h_edge, dst, num_segments=n)
        h = h_dst + h_neigh + h_edge_agg
        return h.reshape(n, H * D)
    h = jnp.maximum(_layernorm(x, axis=-1), 0.0)
    x = x + _L0_gnn_ref(h, edge_attr_128, L0_gnn_W_src, L0_gnn_W_dst, L0_gnn_W_edge, L0_gnn_attn_src, L0_gnn_attn_dst, L0_gnn_attn_edge, src, dst)
    return x

_drawn_inputs = setup_inputs


def setup_inputs(seed=0):
    import zlib

    import numpy as np

    out = dict(_drawn_inputs(seed))
    spreads = {}
    factors = {}
    for name, (base, spread) in spreads.items():
        noise = np.random.default_rng([zlib.crc32(name.encode()), seed]).standard_normal(out[name].shape)
        drawn = base * np.exp(spread * noise) if base else spread * noise
        out[name] = jnp.asarray(drawn.astype(out[name].dtype))
    for name, factor in factors.items():
        out[name] = (out[name] * factor).astype(out[name].dtype)
    return out
```

```python
from contextlib import ExitStack

import concourse.bass as bass
from concourse import mybir

F32 = mybir.dt.float32
I32 = mybir.dt.int32
ALU = mybir.AluOpType
ACT = mybir.ActivationFunctionType
AX = mybir.AxisListType

P = 128
HEADS = 4
DH = 32
G = 2 * HEADS
GC = DH + 1
ROW = P + HEADS
HROW = ROW + HEADS
TILES = 16
HALF = TILES // 2
CHUNK = TILES * P
BIG = 1.0e30
EPS = 1e-5
SLOPE = 0.2
NGRP = 7
LAG = 4
GSEM = 8


def gnn_program(nc, x, src_t, dst_t, dst_runs, half_marks, tile_marks, edge, w_src, w_dst, w_edge, a_src, a_dst, a_edge, out,
                nodes):
    node_tiles = x.shape[0] // P
    groups = node_tiles // NGRP
    chunks = edge.shape[0]
    tiles = chunks * TILES
    halves = 2 * chunks
    pairs = TILES // 2
    wide = (node_tiles + 1) * P
    assert groups * NGRP == node_tiles and chunks % 2 == 1 and chunks >= 5

    table = nc.dram_tensor("table", (node_tiles * P, ROW), F32, kind="Internal").ap()
    edst = nc.dram_tensor("edst", (wide, HEADS), F32, kind="Internal").ap()
    sums = nc.dram_tensor("sums", (wide, G * GC), F32, kind="Internal").ap()

    ctx = ExitStack()
    with ctx:
        def sb(name, shape, dt=F32):
            return ctx.enter_context(nc.sbuf_tensor(name, shape, dt))

        def ps(name):
            return ctx.enter_context(nc.psum_tensor(name, [P, 512], F32))

        def sem(name):
            return ctx.enter_context(nc.semaphore(name))

        ident = sb("ident", [P, P])
        iota_row = sb("iota_row", [P, P])
        iota_i = sb("iota_i", [P, P], I32)
        iota_col = sb("iota_col", [P, 1])
        iota_ci = sb("iota_ci", [P, 1], I32)
        ones8 = sb("ones8", [G, P])
        tile_mask = sb("tile_mask", [P, TILES])
        group_sel = sb("group_sel", [P, G])
        group_sel_t = sb("group_sel_t", [G, P])
        w_in = sb("w_in", [P, 3, P])
        a_in = sb("a_in", [P, 3])
        head_mask = sb("head_mask", [P, HEADS])
        a_diag = sb("a_diag", [P, 3, HEADS])
        w_node = sb("w_node", [P, 2 * ROW])
        w_edge_t = sb("w_edge_t", [P, ROW])
        xn = sb("xn", [P, node_tiles, P])
        centred = sb("centred", [P, NGRP, P])
        squares = sb("squares", [P, NGRP, P])
        stats = sb("stats", [P, 5, NGRP])
        ht = sb("ht", [P, 2, P])
        rows_out = sb("rows_out", [P, node_tiles, ROW])
        edst_out = sb("edst_out", [P, node_tiles + 1, HEADS])
        zeros = sb("zeros", [P, G * GC])
        dst_sb = sb("dst_sb", [P, tiles], I32)
        rel = sb("rel", [P, tiles])
        hm_i = sb("hm_i", [P, 3, halves], I32)
        carry_sel = sb("carry_sel", [P, halves])
        goes_on = sb("goes_on", [P, halves])
        tm_i = sb("tm_i", [G, 2, tiles], I32)
        tm_j = sb("tm_j", [G, 2, tiles], I32)
        tile_keep = sb("tile_keep", [G, 2, tiles])
        idx = sb("idx", [P, 2, TILES], I32)
        rows = sb("rows", [P, 2, TILES, ROW])
        xe = sb("xe", [P, 2, TILES, P])
        runs = sb("runs", [P, 2, 3, P], I32)
        window = sb("window", [P, 2, 2, HEADS])
        hot = sb("hot", [P, 2, TILES, P])
        turned = sb("turned", [P, 2, 4, P])
        he = sb("he", [P, 2, TILES, HROW])
        z = sb("z", [P, TILES, G])
        same = sb("same", [P, 2, P])
        keep = sb("keep", [P, 2, P])
        run_fwd = sb("run_fwd", [P, P])
        run_max = sb("run_max", [P, P])
        ends = sb("ends", [P, 2, TILES])
        across = sb("across", [G, 2 * (TILES + 2)])
        start = sb("start", [P, 2, TILES])
        init = sb("init", [P, 2])
        shifted = sb("shifted", [P, P])
        weights_t = sb("weights_t", [P, P])
        drop = sb("drop", [G, 1])
        rescale = sb("rescale", [G, 1])
        rescale_diag = sb("rescale_diag", [G, G])
        msg = sb("msg", [P, TILES, G, GC])
        carry_in = sb("carry_in", [P, G, GC])
        carry_hot = sb("carry_hot", [P, 2, P])
        agg_sb = sb("agg_sb", [P, 2, G * GC])
        inv = sb("inv", [P, NGRP, G])
        back = xe[:, :, :, :].rearrange("p q t f -> p (q t f)")[:, 0:2 * NGRP * G * GC].rearrange(
            "p (b t g k) -> p b t g k", b=2, t=NGRP, g=G)
        normed = hot[:, :, :, :].rearrange("p q t f -> p (q t f)")[:, 0:NGRP * G * DH].rearrange(
            "p (t g k) -> p t g k", t=NGRP, g=G)

        turn_ps = [ps(f"turn_ps{i}") for i in range(2)]
        proj_ps = [ps(f"proj_ps{i}") for i in range(2)]
        scan_ps = ps("scan_ps")
        wt_ps = ps("wt_ps")
        agg_ps = [ps(f"agg_ps{i}") for i in range(2)]

        names = """weights_in attn_in x_first x_rest marks_in ident_zero ident_done iota_done consts_done zero_done
            w_turned w_ready w_step centred_ready squared var_ready std_ready normed_ready n_turned ht_ready n_proj rows_ready0
            node_rows base_added table_out fill_out node_step marks_ready
            gathered turned_ready turned_out proj_ready he_ready hot_ready z_ready zt_ready ends_ready across_in across_ready
            start_ready shifted_ready drop_ready weights_ready rescale_ready diag_ready factors_ready wt_ready msg_den msg_ready agg_done
            agg_out chain carried sums_out read_back0 read_back1 final_step out_ready out_done""".split()
        S = {n: sem(n) for n in names}
        x_in = [sem(f"x_in{q}") for q in range(2)]
        idx_in = [sem(f"idx_in{q}") for q in range(2)]
        runs_in = [sem(f"runs_in{q}") for q in range(2)]
        window_in = [sem(f"window_in{q}{s}") for q in range(2) for s in range(2)]
        gather_sem = [sem(f"gather{k}") for k in range(GSEM)]

        def wait(eng, s, value):
            if not isinstance(value, int) or value > 0:
                eng.wait_ge(s, value)

        def over_chunks(eng, body):
            body(0, 0)
            body(0, 1)
            with eng.Fori(1, chunks // 2) as i:
                body(i, 0)
                body(i, 1)
            body(chunks // 2, 0)

        def over_groups(eng, body):
            body(0)
            with eng.Fori(1, groups) as g:
                body(g)

        def bc(ap, axis, n):
            a = ap.unsqueeze(axis)
            shape = list(a.shape)
            shape[axis] = n
            return a.to_broadcast(shape)

        block = ctx.enter_context(nc.Block())

        @block.sync
        def _(sp):
            def hold(s, value):
                wait(sp, s, value)
                sp.nop(nofuse=True)

            x_tiles = x.rearrange("(t p) f -> p t f", p=P)
            for k, w in enumerate((w_src, w_dst, w_edge)):
                sp.dma_start(w_in[:, k, :], w).then_inc(S["weights_in"], 16)
            sp.dma_start(xn[:, 0:NGRP, :], x_tiles[:, 0:NGRP, :]).then_inc(S["x_first"], 16)
            sp.dma_start(xn[:, NGRP:node_tiles, :], x_tiles[:, NGRP:node_tiles, :]).then_inc(S["x_rest"], 16)

            def load(i, q):
                c = 2 * i + q
                sp.dma_start(idx[:, q, :], src_t[:, bass.ds(c * TILES, TILES)]).then_inc(idx_in[q], 16)
                sp.dma_start(xe[:, q, :, :], edge[bass.ds(c, 1), :, :].rearrange("a p (t f) -> (a p) t f", t=TILES)
                             ).then_inc(x_in[q], 16)
                sp.dma_start(runs[:, q, :, :], dst_runs[bass.ds(c, 1), :, :].rearrange("a p (k e) -> (a p) k e", k=3)
                             ).then_inc(runs_in[q], 16)

            def load_windows(i, q):
                c = 2 * i + q
                for s in range(2):
                    first = sp.value_load(hm_i[0:1, 0, bass.ds(2 * c + s, 1)], min_val=0, max_val=nodes)
                    sp.dma_start(window[:, q, s, :], edst[bass.ds(first, P), :]).then_inc(window_in[2 * q + s], 16)

            load(0, 0)
            load(0, 1)
            table_tiles = table.rearrange("(t p) f -> p t f", p=P)
            edst_tiles = edst.rearrange("(t p) f -> p t f", p=P)

            def store_rows(g):
                hold(S["node_rows"], (g + 1) * NGRP)
                sp.dma_start(table_tiles[:, bass.ds(g * NGRP, NGRP), :], rows_out[:, bass.ds(g * NGRP, NGRP), :]
                             ).then_inc(S["table_out"], 16)

            over_groups(sp, store_rows)
            sp.wait_ge(S["base_added"], node_tiles)
            sp.dma_start(edst_tiles, edst_out[:, :, :]).then_inc(S["table_out"], 16)
            sp.wait_ge(S["table_out"], 16 * (groups + 1))
            sp.wait_ge(S["marks_in"], 16 * 8)
            load_windows(0, 0)
            load_windows(0, 1)
            sp.wait_ge(S["fill_out"], 16)

            def store_windows(d):
                for s in range(2):
                    u = 2 * d + s
                    first = sp.value_load(hm_i[0:1, 0, bass.ds(u, 1)], min_val=0, max_val=nodes)
                    hold(S["agg_out"], u + 1)
                    hold(S["sums_out"], u * 16)
                    sp.dma_start(sums[bass.ds(first, P), :], agg_sb[:, s, :]).then_inc(S["sums_out"], 16)

            def step(i, q):
                c = 2 * i + q
                if isinstance(c, int) and c < 2:
                    return
                hold(S["turned_ready"], (c - 1) * pairs)
                hold(S["proj_ready"], (c - 1) * pairs)
                hold(S["gathered"], c - 1)
                hold(S["z_ready"], c - 1)
                load(i, q)
                load_windows(i, q)
                store_windows(c - 2)

            over_chunks(sp, step)
            store_windows(chunks - 2)
            store_windows(chunks - 1)
            sums_tiles = sums.rearrange("(t p) (g k) -> p t g k", p=P, k=GC)
            out_tiles = out.rearrange("(t p) f -> p t f", p=P)
            sp.wait_ge(S["sums_out"], 16 * halves)
            for g in range(groups + 1):
                if g < groups:
                    if g >= 2:
                        sp.wait_ge(S["final_step"], 3 * (g - 2) + 3)
                    sp.dma_start(back[:, g % 2, :, :, :].rearrange("p t g k -> p t (g k)"),
                                 sums_tiles[:, g * NGRP:(g + 1) * NGRP].rearrange("p t g k -> p t (g k)")
                                 ).then_inc(S[f"read_back{g % 2}"], 16)
                if g >= 1:
                    t0, t1 = (g - 1) * NGRP, g * NGRP
                    sp.wait_ge(S["out_ready"], g)
                    sp.dma_start(out_tiles[:, t0:t1, :], xn[:, t0:t1, :]).then_inc(S["out_done"], 16)
            sp.wait_ge(S["out_done"], 16 * groups)

        @block.gpsimd
        def _(g_):
            g_.memset(ident[:, :], 0.0).then_inc(S["ident_zero"], 1)
            g_.iota(iota_i[:, :], pattern=[[1, P]], base=0, channel_multiplier=0).then_inc(S["iota_done"], 1)
            g_.iota(iota_ci[:, :], pattern=[[0, 1]], base=0, channel_multiplier=1).then_inc(S["iota_done"], 1)
            g_.wait_ge(S["ident_zero"], 1)
            g_.affine_select(out=ident[:, :], in_=ident[:, :], compare_op=ALU.not_equal, fill=1.0, base=0,
                             pattern=[[-1, P]], channel_multiplier=1).then_inc(S["ident_done"], 1)
            g_.wait_ge(S["table_out"], 16 * (groups + 1))
            per = TILES // GSEM

            def confirm(c, t):
                g_.wait_ge(gather_sem[t % GSEM], 16 * (per * c + t // GSEM + 1))

            def step(i, q):
                c = 2 * i + q
                g_.wait_ge(idx_in[q], 16 * (i + 1))
                wait(g_, S["msg_ready"], 2 * (c - 1))
                for t in range(TILES):
                    if t >= LAG:
                        confirm(c, t - LAG)
                    elif not (isinstance(c, int) and c == 0):
                        confirm(c - 1, TILES - LAG + t)
                        if t == LAG - 1:
                            g_.sem_inc(S["gathered"], 1)
                    g_.nop(nofuse=True)
                    g_.indirect_dma_start(out=rows[:, q, t, :], out_offset=None, in_=table[:, :],
                                          in_offset=bass.IndirectOffsetOnAxis(ap=idx[:, q, t:t + 1], axis=0)
                                          ).then_inc(gather_sem[t % GSEM], 16)

            over_chunks(g_, step)
            for t in range(TILES - LAG, TILES):
                confirm(chunks - 1, t)
            g_.sem_inc(S["gathered"], 1)

        @block.tensor
        def _(pe):
            pe.wait_ge(S["weights_in"], 48)
            pe.wait_ge(S["ident_done"], 1)
            pe.wait_ge(S["w_step"], 3)
            for k in range(3):
                pe.transpose(agg_ps[0][:, k * P:(k + 1) * P], w_in[:, k, :], ident[:, :])
            for k in range(3):
                last = pe.matmul(agg_ps[1][:, k * HEADS:(k + 1) * HEADS], w_in[:, k, :], a_diag[:, k, :],
                                 start=True, stop=True)
            last.then_inc(S["w_turned"], 1)

            def node_group(g):
                for j in range(NGRP):
                    n = g * NGRP + j
                    if j == 0:
                        pe.wait_ge(S["normed_ready"], g + 1)
                    b = j % 2
                    wait(pe, S["ht_ready"], n)
                    pe.transpose(turn_ps[b][:, 0:P], centred[:, j, :], ident[:, :]).then_inc(S["n_turned"], 1)
                    if j == 0 and isinstance(g, int) and g == 0:
                        pe.wait_ge(S["w_ready"], 1)
                    pe.wait_ge(S["ht_ready"], n + 1)
                    wait(pe, S["node_rows"], n - 1 if j else n)
                    wait(pe, S["base_added"], n - 1 if j else n)
                    pe.matmul(proj_ps[b][:, 0:2 * ROW], ht[:, b, :], w_node[:, :], start=True, stop=True
                              ).then_inc(S["n_proj"], 1)

            over_groups(pe, node_group)

            def turn(i, q, n):
                c = 2 * i + q
                k = c * pairs + n
                wait(pe, S["turned_out"], k - 1)
                for j in range(2):
                    pe.transpose(turn_ps[n % 2][:, j * P:(j + 1) * P], xe[:, q, 2 * n + j, :], ident[:, :])
                for j in range(2):
                    last = pe.transpose(turn_ps[n % 2][:, (2 + j) * P:(3 + j) * P], hot[:, q, 2 * n + j, :], ident[:, :])
                last.then_inc(S["turned_ready"], 1)

            def project(i, q, n):
                c = 2 * i + q
                k = c * pairs + n
                pe.wait_ge(S["turned_out"], k + 1)
                wait(pe, S["he_ready"], k - 1)
                if n == 0 or n == pairs // 2:
                    pe.wait_ge(window_in[2 * q + n // (pairs // 2)], 16 * (i + 1))
                for j in range(2):
                    o = j * HROW
                    pe.matmul(proj_ps[n % 2][:, o:o + ROW], turned[:, n % 2, j, :], w_edge_t[:, :], start=True, stop=True)
                    last = pe.matmul(proj_ps[n % 2][:, o + ROW:o + HROW], turned[:, n % 2, 2 + j, :],
                                     window[:, q, n // (pairs // 2), :], start=True, stop=True)
                last.then_inc(S["proj_ready"], 1)

            def turn_logits(d):
                pe.wait_ge(S["z_ready"], d + 1)
                pe.transpose(scan_ps[:, 0:P], z[:, :, :].rearrange("p t g -> p (t g)"), ident[:, :]
                             ).then_inc(S["zt_ready"], 1)

            def gather_ends(d):
                pe.wait_ge(S["ends_ready"], d + 1)
                pe.matmul(scan_ps[0:G, P:P + 2 * TILES], group_sel[:, :], ends[:, :, :].rearrange("p a t -> p (a t)"),
                          start=True, stop=True).then_inc(S["across_in"], 1)

            def spread_starts(d):
                pe.wait_ge(S["across_ready"], d + 1)
                pe.matmul(scan_ps[:, P + 2 * TILES:P + 4 * TILES], group_sel_t[:, :],
                          across[:, :].rearrange("g (a t) -> g a t", a=2)[:, :, 0:TILES],
                          start=True, stop=True).then_inc(S["start_ready"], 1)

            def turn_weights(d):
                pe.wait_ge(S["diag_ready"], d + 1)
                pe.matmul(scan_ps[:, P + 4 * TILES:P + 4 * TILES + G], ones8[:, :], rescale_diag[:, :], start=True,
                          stop=True).then_inc(S["factors_ready"], 1)
                pe.wait_ge(S["weights_ready"], d + 1)
                pe.transpose(wt_ps[:, 0:P], weights_t[:, :], ident[:, :]).then_inc(S["wt_ready"], 1)

            def aggregate(i, q):
                d = 2 * i + q
                for s in range(2):
                    u = 2 * d + s
                    pe.wait_ge(S["msg_ready"], u + 1)
                    wait(pe, S["agg_out"], u - 1)
                    for t in range(s * HALF, (s + 1) * HALF):
                        pe.matmul(agg_ps[s][:, 0:G * GC], hot[:, q, t, :], msg[:, t, :, :].rearrange("p g k -> p (g k)"),
                                  start=(t == s * HALF), stop=False)
                    if s == 0:
                        pe.wait_ge(S["carried"], d + 1)
                        carry = carry_in[:, :, :].rearrange("p g k -> p (g k)")
                    else:
                        pe.wait_ge(S["agg_out"], u)
                        carry = agg_sb[:, 0, :]
                    pe.matmul(agg_ps[s][:, 0:G * GC], carry_hot[:, s, :], carry, start=False, stop=True
                              ).then_inc(S["agg_done"], 1)

            def front(i, q, after):
                pe.wait_ge(x_in[q], 16 * (i + 1))
                for n in range(pairs):
                    if n % (pairs // 2) == 0:
                        c = 2 * i + q
                        pe.wait_ge(S["hot_ready"], 2 * c + n // (pairs // 2) + 1)
                    turn(i, q, n)
                    if n:
                        project(i, q, n - 1)
                    if n in after:
                        after[n]()
                project(i, q, pairs - 1)

            def step(i, q):
                c = 2 * i + q
                if isinstance(c, int) and c == 0:
                    front(i, q, {})
                    return
                front(i, q, {1: lambda: turn_logits(c - 1), 2: lambda: gather_ends(c - 1), 3: lambda: spread_starts(c - 1),
                             5: lambda: turn_weights(c - 1)})
                aggregate(*(prev(i, q)))

            def prev(i, q):
                return (i, 0) if q else (i - 1, 1)

            over_chunks(pe, step)
            for part in (turn_logits, gather_ends, spread_starts, turn_weights):
                part(chunks - 1)
            aggregate(chunks // 2, 0)

        @block.scalar
        def _(act):
            for k, a in enumerate((a_src, a_dst, a_edge)):
                act.dma_start(a_in[:, k:k + 1], a.rearrange("h (d o) -> (h d) o", o=1)).then_inc(S["attn_in"], 16)
            act.dma_start(dst_sb[:, :], dst_t).then_inc(S["marks_in"], 16)
            for k in range(3):
                act.dma_start(hm_i[:, k, :], half_marks[k:k + 1, :].to_broadcast([P, halves])).then_inc(S["marks_in"], 16)
            for k in range(2):
                act.dma_start(tm_i[:, k, :], tile_marks[2 * k:2 * k + 1, :].to_broadcast([G, tiles])
                              ).then_inc(S["marks_in"], 16)
                act.dma_start(tm_j[:, k, :], tile_marks[2 * k + 1:2 * k + 2, :].to_broadcast([G, tiles])
                              ).then_inc(S["marks_in"], 16)
            act.wait_ge(S["zero_done"], 1)
            act.dma_start(sums.rearrange("(t p) f -> p t f", p=P), bc(zeros[:, :], 1, node_tiles + 1)
                          ).then_inc(S["fill_out"], 16)
            act.wait_ge(S["w_turned"], 1)
            act.activation(w_node[:, 0:P], agg_ps[0][:, 0:P], ACT.Copy)
            act.activation(w_node[:, ROW:ROW + P], agg_ps[0][:, P:2 * P], ACT.Copy)
            act.activation(w_edge_t[:, 0:P], agg_ps[0][:, 2 * P:3 * P], ACT.Copy)
            act.activation(w_node[:, P:ROW], agg_ps[1][:, 0:HEADS], ACT.Copy)
            act.activation(w_node[:, ROW + P:2 * ROW], agg_ps[1][:, HEADS:2 * HEADS], ACT.Copy)
            act.activation(w_edge_t[:, P:ROW], agg_ps[1][:, 2 * HEADS:3 * HEADS], ACT.Copy).then_inc(S["w_ready"], 1)

            def node_group(g):
                act.wait_ge(S["centred_ready"], g + 1)
                act.activation(squares[:, :, :], centred[:, :, :], ACT.Square).then_inc(S["squared"], 1)
                act.wait_ge(S["var_ready"], g + 1)
                act.activation(stats[:, 3, :], stats[:, 2, :], ACT.Sqrt).then_inc(S["std_ready"], 1)
                for j in range(NGRP):
                    n = g * NGRP + j
                    b = j % 2
                    act.wait_ge(S["n_turned"], n + 1)
                    wait(act, S["n_proj"], n - 1 if j else n)
                    act.activation(ht[:, b, :], turn_ps[b][:, 0:P], ACT.Relu).then_inc(S["ht_ready"], 1)
                    act.wait_ge(S["n_proj"], n + 1)
                    act.activation(rows_out[:, bass.ds(n, 1), :].rearrange("p a f -> p (a f)"), proj_ps[b][:, 0:ROW],
                                   ACT.Copy).then_inc(S["node_rows"], 1)

            over_groups(act, node_group)

            def turned_copy(i, q, n):
                k = (2 * i + q) * pairs + n
                act.wait_ge(S["turned_ready"], k + 1)
                wait(act, S["proj_ready"], k - 1)
                act.activation(turned[:, n % 2, :, :], turn_ps[n % 2][:, :].rearrange("p (a f) -> p a f", a=4), ACT.Copy
                               ).then_inc(S["turned_out"], 1)

            def he_copy(i, q, n):
                c = 2 * i + q
                k = c * pairs + n
                if n == 0:
                    wait(act, S["msg_ready"], 2 * (c - 1))
                act.wait_ge(S["proj_ready"], k + 1)
                act.activation(he[:, q, 2 * n:2 * n + 2, :],
                               proj_ps[n % 2][:, 0:2 * HROW].rearrange("p (a f) -> p a f", a=2), ACT.Copy
                               ).then_inc(S["he_ready"], 1)

            def exps(d):
                act.wait_ge(S["drop_ready"], d + 1)
                wait(act, S["diag_ready"], d)
                act.activation(rescale[:, :], drop[:, :], ACT.Exp).then_inc(S["rescale_ready"], 1)
                act.wait_ge(S["shifted_ready"], d + 1)
                wait(act, S["wt_ready"], d)
                act.activation(weights_t[:, :], shifted[:, :], ACT.Exp).then_inc(S["weights_ready"], 1)

            def put_weights(d):
                act.wait_ge(S["wt_ready"], d + 1)
                wait(act, S["agg_done"], 2 * d)
                act.activation(msg[:, :, :, DH:GC].rearrange("p t g o -> p (t g) o"),
                               wt_ps[:, 0:P].rearrange("p (a o) -> p a o", o=1), ACT.Copy
                               ).then_inc(S["msg_den"], 1)

            def windows_out(d):
                for s in range(2):
                    u = 2 * d + s
                    act.wait_ge(S["agg_done"], u + 1)
                    wait(act, S["sums_out"], 16 * (u - 1))
                    if s == 1:
                        act.wait_ge(S["carried"], d + 1)
                    act.activation(agg_sb[:, s, :], agg_ps[s][:, 0:G * GC], ACT.Copy).then_inc(S["agg_out"], 1)

            def step(i, q):
                c = 2 * i + q
                back_due = not (isinstance(c, int) and c == 0)
                for n in range(pairs):
                    turned_copy(i, q, n)
                    if n:
                        he_copy(i, q, n - 1)
                    if n == 4 and back_due:
                        exps(c - 1)
                    if n == 6 and back_due:
                        put_weights(c - 1)
                he_copy(i, q, pairs - 1)
                if back_due:
                    windows_out(c - 1)

            over_chunks(act, step)
            exps(chunks - 1)
            put_weights(chunks - 1)
            windows_out(chunks - 1)

        @block.vector
        def _(v):
            v.memset(zeros[:, :], 0.0).then_inc(S["zero_done"], 1)
            v.memset(edst_out[:, node_tiles, :], 0.0).then_inc(S["consts_done"], 1)
            v.memset(carry_hot[:, :, :], 0.0).then_inc(S["consts_done"], 1)
            v.memset(agg_sb[:, 1, :], 0.0).then_inc(S["consts_done"], 1)
            v.memset(ones8[:, :], 1.0).then_inc(S["consts_done"], 1)
            v.memset(across[:, :], -BIG).then_inc(S["consts_done"], 1)
            v.memset(head_mask[:, :], 0.0).then_inc(S["w_step"], 1)
            v.wait_ge(S["w_step"], 1)
            for h in range(HEADS):
                last = v.memset(head_mask[h * DH:(h + 1) * DH, h:h + 1], 1.0)
            last.then_inc(S["w_step"], 1)
            v.wait_ge(S["w_step"], 2)
            v.wait_ge(S["attn_in"], 48)
            v.tensor_tensor(a_diag[:, :, :], bc(head_mask[:, :], 1, 3), bc(a_in[:, :], 2, HEADS), ALU.mult
                            ).then_inc(S["w_step"], 1)
            v.wait_ge(S["iota_done"], 2)
            v.tensor_copy(iota_row[:, :], iota_i[:, :]).then_inc(S["consts_done"], 1)
            v.tensor_copy(iota_col[:, :], iota_ci[:, :]).then_inc(S["consts_done"], 1)
            v.wait_ge(S["ident_done"], 1)
            v.tensor_reduce(tile_mask[:, :], ident[:, :].rearrange("p (t g) -> p t g", g=G), AX.X, ALU.add
                            ).then_inc(S["consts_done"], 1)
            v.tensor_reduce(group_sel[:, :], ident[:, :].rearrange("p (t g) -> p g t", g=G), AX.X, ALU.add
                            ).then_inc(S["consts_done"], 1)
            v.tensor_copy(group_sel_t[:, :].rearrange("c (t g) -> c t g", g=G), bc(ident[0:G, 0:G], 1, TILES)
                          ).then_inc(S["consts_done"], 1)

            nsteps = 4

            def node_group(g):
                base = g * nsteps
                tiles_of = xn[:, bass.ds(g * NGRP, NGRP), :]
                wait(v, S["n_turned"], g * NGRP)
                v.tensor_reduce(stats[:, 0, :], tiles_of, AX.X, ALU.add).then_inc(S["node_step"], 1)
                v.wait_ge(S["node_step"], base + 1)
                v.tensor_scalar(stats[:, 1, :], stats[:, 0, :], 1.0 / P, None, ALU.mult).then_inc(S["node_step"], 1)
                v.wait_ge(S["node_step"], base + 2)
                v.tensor_tensor(centred[:, :, :], tiles_of, bc(stats[:, 1, :], 2, P), ALU.subtract
                                ).then_inc(S["centred_ready"], 1)
                v.wait_ge(S["squared"], g + 1)
                v.tensor_reduce(stats[:, 0, :], squares[:, :, :], AX.X, ALU.add).then_inc(S["node_step"], 1)
                v.wait_ge(S["node_step"], base + 3)
                v.tensor_scalar(stats[:, 2, :], stats[:, 0, :], 1.0 / P, EPS, ALU.mult, ALU.add).then_inc(S["var_ready"], 1)
                v.wait_ge(S["std_ready"], g + 1)
                v.reciprocal(stats[:, 4, :], stats[:, 3, :]).then_inc(S["node_step"], 1)
                v.wait_ge(S["node_step"], base + 4)
                v.wait_ge(S["centred_ready"], g + 1)
                v.tensor_tensor(centred[:, :, :], centred[:, :, :], bc(stats[:, 4, :], 2, P), ALU.mult
                                ).then_inc(S["normed_ready"], 1)
                for j in range(NGRP):
                    n = g * NGRP + j
                    v.wait_ge(S["node_rows"], n + 1)
                    v.tensor_copy(edst_out[:, bass.ds(n, 1), :].rearrange("p a f -> p (a f)"),
                                  proj_ps[j % 2][:, ROW + P:2 * ROW])
                    row = xn[:, bass.ds(n, 1), :].rearrange("p a f -> p (a f)")
                    v.tensor_tensor(row, row, proj_ps[j % 2][:, ROW:ROW + P], ALU.add).then_inc(S["base_added"], 1)

            v.wait_ge(S["x_first"], 16)
            node_group(0)
            v.wait_ge(S["x_rest"], 16)
            with v.Fori(1, groups) as g:
                node_group(g)

            v.wait_ge(S["marks_in"], 16 * 8)
            v.tensor_tensor(rel[:, :].rearrange("p (u t) -> p u t", t=HALF), dst_sb[:, :].rearrange("p (u t) -> p u t", t=HALF),
                            bc(hm_i[:, 0, :], 2, HALF), ALU.subtract).then_inc(S["marks_ready"], 1)
            v.wait_ge(S["consts_done"], 10)
            v.scalar_tensor_tensor(out=carry_sel[:, :], in0=hm_i[:, 2, :], scalar=iota_col[:, 0:1], in1=hm_i[:, 0, :],
                                   op0=ALU.add, op1=ALU.is_equal).then_inc(S["marks_ready"], 1)
            v.tensor_tensor(tile_keep[:, :, :], tm_i[:, :, :], tm_j[:, :, :], ALU.is_equal).then_inc(S["marks_ready"], 1)
            v.tensor_tensor(goes_on[:, :], hm_i[:, 1, :], hm_i[:, 0, :], ALU.is_equal).then_inc(S["marks_ready"], 1)
            v.wait_ge(S["marks_ready"], 4)
            v.tensor_tensor(carry_sel[:, :], carry_sel[:, :], goes_on[:, :], ALU.mult).then_inc(S["marks_ready"], 1)
            v.tensor_scalar(tile_keep[:, :, :], tile_keep[:, :, :], -0.5, 2 * BIG, ALU.add, ALU.mult
                            ).then_inc(S["marks_ready"], 1)
            v.wait_ge(S["marks_ready"], 6)

            def one_hot(i, q):
                c = 2 * i + q
                for s in range(2):
                    wait(v, S["agg_done"], 2 * (c - 1))
                    v.tensor_tensor(hot[:, q, s * HALF:(s + 1) * HALF, :], bc(iota_row[:, :], 1, HALF),
                                    bc(rel[:, bass.ds((2 * c + s) * HALF, HALF)], 2, P), ALU.is_equal
                                    ).then_inc(S["hot_ready"], 1)

            links = 11

            def softmax(i, q):
                d = 2 * i + q
                done = [0]

                def link(ins):
                    done[0] += 1
                    ins.then_inc(S["chain"], 1)
                    v.wait_ge(S["chain"], d * links + done[0])

                v.wait_ge(runs_in[q], 16 * (i + 1))
                link(v.tensor_tensor(same[:, :, :], bc(runs[:, q, 0, :], 1, 2), runs[:, q, 1:3, :], ALU.is_equal))
                link(v.tensor_scalar(keep[:, :, :], same[:, :, :], -0.5, 2 * BIG, ALU.add, ALU.mult))
                wait(v, S["agg_done"], 2 * d)
                link(v.tensor_copy(carry_hot[:, :, 0], carry_sel[:, bass.ds(2 * d, 2)]))
                v.wait_ge(S["he_ready"], (d + 1) * pairs)
                v.wait_ge(S["gathered"], d + 1)
                wait(v, S["zt_ready"], d)
                v.tensor_tensor(z[:, :, 0:HEADS], rows[:, q, :, P:ROW], he[:, q, :, ROW:HROW], ALU.add)
                link(v.tensor_tensor(z[:, :, HEADS:G], he[:, q, :, P:ROW], he[:, q, :, ROW:HROW], ALU.add))
                v.scalar_tensor_tensor(out=z[:, :, :], in0=z[:, :, :], scalar=SLOPE, in1=z[:, :, :],
                                       op0=ALU.mult, op1=ALU.max).then_inc(S["z_ready"], 1)
                v.wait_ge(S["zt_ready"], d + 1)
                logits = scan_ps[:, 0:P]
                link(v.tensor_tensor_scan(run_fwd[:, :], keep[:, 0, :], logits, -BIG, ALU.min, ALU.max))
                link(v.tensor_tensor_scan(run_max[:, ::-1], keep[:, 1, ::-1], run_fwd[:, ::-1], -BIG, ALU.min, ALU.max))
                v.tensor_scalar(ends[:, 0, :], tile_mask[:, :], run_fwd[:, P - 1:P], None, ALU.mult)
                v.tensor_scalar(ends[:, 1, :], tile_mask[:, :], run_max[:, 0:1], None, ALU.mult).then_inc(S["ends_ready"], 1)
                W = TILES + 2
                wait(v, S["start_ready"], d)
                link(v.tensor_copy(across[:, 0:1], across[:, TILES:TILES + 1]))
                v.wait_ge(S["across_in"], d + 1)
                v.tensor_tensor_scan(across[:, 1:TILES + 1], tile_keep[:, 0, bass.ds(d * TILES, TILES)],
                                     scan_ps[0:G, P:P + TILES], across[:, 0:1], ALU.min, ALU.max)
                v.tensor_tensor_scan(across[:, W - 1:W - 1 + TILES][:, ::-1],
                                     tile_keep[:, 1, bass.ds(d * TILES, TILES)],
                                     scan_ps[0:G, P + TILES:P + 2 * TILES][:, ::-1], -BIG, ALU.min, ALU.max
                                     ).then_inc(S["across_ready"], 1)
                v.wait_ge(S["start_ready"], d + 1)
                link(v.tensor_tensor(start[:, :, :],
                                     scan_ps[:, P + 2 * TILES:P + 4 * TILES].rearrange("p (a t) -> p a t", a=2),
                                     bc(tile_mask[:, :], 1, 2), ALU.mult))
                link(v.tensor_reduce(init[:, :], start[:, :, :], AX.X, ALU.add))
                link(v.tensor_tensor_scan(run_fwd[:, :], keep[:, 0, :], logits, init[:, 0:1], ALU.min, ALU.max))
                link(v.tensor_tensor_scan(run_max[:, ::-1], keep[:, 1, ::-1], run_fwd[:, ::-1], init[:, 1:2],
                                          ALU.min, ALU.max))
                wait(v, S["rescale_ready"], d)
                v.tensor_scalar(drop[:, :], across[:, 0:1], run_max[0:G, 0:1], 0.0, ALU.subtract, ALU.min
                                ).then_inc(S["drop_ready"], 1)
                wait(v, S["weights_ready"], d)
                v.tensor_tensor(shifted[:, :], logits, run_max[:, :], ALU.subtract).then_inc(S["shifted_ready"], 1)
                v.wait_ge(S["rescale_ready"], d + 1)
                wait(v, S["factors_ready"], d)
                v.tensor_scalar(rescale_diag[:, :], ident[0:G, 0:G], rescale[:, 0:1], None, ALU.mult
                                ).then_inc(S["diag_ready"], 1)
                v.wait_ge(S["factors_ready"], d + 1)
                wait(v, S["agg_out"], 2 * d)
                wait(v, S["agg_done"], 2 * d)
                v.tensor_tensor(carry_in[:, :, :], agg_sb[:, 1, :].rearrange("p (g k) -> p g k", k=GC),
                                bc(scan_ps[:, P + 4 * TILES:P + 4 * TILES + G], 2, GC), ALU.mult).then_inc(S["carried"], 1)
                v.wait_ge(S["msg_den"], d + 1)
                for s in range(2):
                    a, b = s * HALF, (s + 1) * HALF
                    w = msg[:, a:b, :, DH:GC]
                    v.tensor_tensor(msg[:, a:b, 0:HEADS, 0:DH],
                                    rows[:, q, a:b, 0:P].rearrange("p t (h k) -> p t h k", k=DH),
                                    w[:, :, 0:HEADS, :].to_broadcast([P, HALF, HEADS, DH]), ALU.mult)
                    v.tensor_tensor(msg[:, a:b, HEADS:G, 0:DH],
                                    he[:, q, a:b, 0:P].rearrange("p t (h k) -> p t h k", k=DH),
                                    w[:, :, HEADS:G, :].to_broadcast([P, HALF, HEADS, DH]), ALU.mult
                                    ).then_inc(S["msg_ready"], 1)
                assert done[0] == links, done[0]

            def step(i, q):
                c = 2 * i + q
                one_hot(i, q)
                if not (isinstance(c, int) and c == 0):
                    softmax(*((i, 0) if q else (i - 1, 1)))

            over_chunks(v, step)
            softmax(chunks // 2, 0)

            for g in range(groups):
                v.wait_ge(S[f"read_back{g % 2}"], 16 * (g // 2 + 1))
                v.tensor_scalar(inv[:, :, :], back[:, g % 2, :, :, DH], 0.5, None, ALU.max).then_inc(S["final_step"], 1)
                v.wait_ge(S["final_step"], 3 * g + 1)
                v.reciprocal(inv[:, :, :], inv[:, :, :]).then_inc(S["final_step"], 1)
                v.wait_ge(S["final_step"], 3 * g + 2)
                v.tensor_tensor(normed[:, :, :, :].rearrange("p t g k -> p (t g) k"),
                                back[:, g % 2, :, :, 0:DH].rearrange("p t g k -> p (t g) k"),
                                bc(inv[:, :, :].rearrange("p t g -> p (t g)"), 2, DH), ALU.mult).then_inc(S["final_step"], 1)
                v.wait_ge(S["final_step"], 3 * g + 3)
                rows_g = xn[:, g * NGRP:(g + 1) * NGRP, :]
                halves_n = normed[:, :, :, :].rearrange("p t (b h) k -> p t b (h k)", b=2)
                v.tensor_tensor(rows_g, rows_g, halves_n[:, :, 0, :], ALU.add).then_inc(S["base_added"], 1)
                v.wait_ge(S["base_added"], node_tiles + g + 1)
                v.tensor_tensor(rows_g, rows_g, halves_n[:, :, 1, :], ALU.add).then_inc(S["out_ready"], 1)


def kernel(**inputs):
    import numpy as np
    import concourse.bacc as bacc
    from concourse.bass_utils import run_bass_kernel_spmd

    a = {k: np.asarray(v) for k, v in inputs.items()}
    n, e = a["x"].shape[0], a["src"].shape[0]
    node_rows = -(-n // (P * NGRP)) * P * NGRP
    chunks = -(-e // CHUNK)
    edges = chunks * CHUNK
    x = np.zeros((node_rows, P), np.float32)
    x[:n] = a["x"]
    src = np.zeros(edges, np.int32)
    src[:e] = a["src"]
    dst = np.full(edges + 2, n, np.int32)
    dst[0] = -1
    dst[1:e + 1] = a["dst"]
    dst[edges + 1] = -1
    here, before, after = dst[1:-1], dst[:-2], dst[2:]
    edge = np.zeros((edges, P), np.float32)
    edge[:e] = a["edge_attr_128"]
    edge = np.ascontiguousarray(edge.reshape(chunks, TILES, P, P).transpose(0, 2, 1, 3)).reshape(chunks, P, TILES * P)
    runs = np.stack([here, before, after], 0).reshape(3, chunks, TILES, 1, P)
    runs = np.ascontiguousarray(np.broadcast_to(runs, (3, chunks, TILES, G, P)).transpose(1, 2, 3, 0, 4))
    step = HALF * P
    first = here[::step]
    none = np.full(1, -1, np.int32)
    half_marks = np.stack([first, before[::step], np.concatenate([none, first[:-1]])])
    t_first, t_last = here[::P], here[P - 1::P]
    turn_back = lambda m: m.reshape(chunks, TILES)[:, ::-1].reshape(-1)
    tile_marks = np.stack([t_last, np.concatenate([none, t_last[:-1]]),
                           turn_back(t_first), turn_back(np.concatenate([t_first[1:], none]))])
    arrays = {
        "x": x, "src_t": np.ascontiguousarray(src.reshape(-1, P).T), "dst_t": np.ascontiguousarray(here.reshape(-1, P).T),
        "dst_runs": runs.reshape(chunks, P, 3 * P), "half_marks": np.ascontiguousarray(half_marks),
        "tile_marks": np.ascontiguousarray(tile_marks), "edge": edge,
        "w_src": a["L0_gnn_W_src"], "w_dst": a["L0_gnn_W_dst"], "w_edge": a["L0_gnn_W_edge"],
        "a_src": a["L0_gnn_attn_src"], "a_dst": a["L0_gnn_attn_dst"], "a_edge": a["L0_gnn_attn_edge"],
    }
    nc = bacc.Bacc("TRN2", target_bir_lowering=False, num_devices=1)
    aps = [nc.dram_tensor(k, v.shape, mybir.dt.from_np(v.dtype), kind="ExternalInput").ap() for k, v in arrays.items()]
    out = nc.dram_tensor("out", (node_rows, P), F32, kind="ExternalOutput").ap()
    gnn_program(nc, *aps, out, n)
    got = run_bass_kernel_spmd(nc, [arrays], core_ids=[0])
    return got.results[0]["out"][:n]
```

```python
from contextlib import ExitStack

import concourse.bass as bass
from concourse import mybir

F32 = mybir.dt.float32
I32 = mybir.dt.int32
ALU = mybir.AluOpType
ACT = mybir.ActivationFunctionType
AX = mybir.AxisListType

P = 128
HEADS = 4
DH = 32
G = 2 * HEADS
GC = DH + 1
ROW = P + HEADS
HROW = ROW + HEADS
TILES = 16
HALF = TILES // 2
CHUNK = TILES * P
BIG = 1.0e30
EPS = 1e-5
SLOPE = 0.2
NGRP = 7
BUFS = 3
LAG = 4
GSEM = 8


def gnn_program(nc, x, src_t, dst_t, dst_runs, half_marks, tile_marks, edge, w_src, w_dst, w_edge, a_src, a_dst, a_edge, out,
                nodes):
    node_tiles = x.shape[0] // P
    groups = node_tiles // NGRP
    chunks = edge.shape[0]
    tiles = chunks * TILES
    halves = 2 * chunks
    pairs = TILES // 2
    quads = TILES // 4
    wide = (node_tiles + 1) * P
    table_stores = 2 * groups + 1
    assert groups * NGRP == node_tiles and groups >= 4 and chunks >= 3 * BUFS

    table = nc.dram_tensor("table", (node_tiles * P, ROW), F32, kind="Internal").ap()
    edst = nc.dram_tensor("edst", (wide, HEADS), F32, kind="Internal").ap()
    sums = nc.dram_tensor("sums", (wide, G * GC), F32, kind="Internal").ap()

    ctx = ExitStack()
    with ctx:
        def sb(name, shape, dt=F32):
            return ctx.enter_context(nc.sbuf_tensor(name, shape, dt))

        def ps(name):
            return ctx.enter_context(nc.psum_tensor(name, [P, 512], F32))

        def sem(name):
            return ctx.enter_context(nc.semaphore(name))

        ident = sb("ident", [P, P])
        iota_row = sb("iota_row", [P, P])
        iota_i = sb("iota_i", [P, P], I32)
        iota_col = sb("iota_col", [P, 1])
        iota_ci = sb("iota_ci", [P, 1], I32)
        ones8 = sb("ones8", [G, P])
        tile_mask = sb("tile_mask", [P, TILES])
        group_sel = sb("group_sel", [P, G])
        group_sel_t = sb("group_sel_t", [G, P])
        w_in = sb("w_in", [P, 3, P])
        a_in = sb("a_in", [P, 3])
        head_mask = sb("head_mask", [P, HEADS])
        a_diag = sb("a_diag", [P, 3, HEADS])
        w_node = sb("w_node", [P, 2 * ROW])
        w_edge_t = sb("w_edge_t", [P, ROW])
        xn = sb("xn", [P, node_tiles, P])
        normal = sb("normal", [P, 2, NGRP, P])
        bn = sb("bn", [P, 2, NGRP, 6])
        moments = sb("moments", [P, 2, NGRP, 2])
        spread = sb("spread", [P, 2, 3, NGRP])
        ht = sb("ht", [P, 2, P])
        zeros = sb("zeros", [P, G * GC])
        dst_sb = sb("dst_sb", [P, tiles], I32)
        rel = sb("rel", [P, tiles])
        hm_i = sb("hm_i", [P, 3, halves], I32)
        carry_sel = sb("carry_sel", [P, halves])
        goes_on = sb("goes_on", [P, halves])
        tm_i = sb("tm_i", [G, 2, tiles], I32)
        tm_j = sb("tm_j", [G, 2, tiles], I32)
        tile_keep = sb("tile_keep", [G, 2, tiles])
        idx = sb("idx", [P, BUFS, TILES], I32)
        rows = sb("rows", [P, BUFS, TILES, ROW])
        xe = sb("xe", [P, BUFS, TILES, P])
        runs = sb("runs", [P, BUFS, 3, P], I32)
        window = sb("window", [P, BUFS, 2, HEADS])
        hot_memory = sb("hot_memory", [P, max(BUFS * TILES * P, node_tiles * HROW)])
        hot = hot_memory[:, 0:BUFS * TILES * P].rearrange("p (q t f) -> p q t f", q=BUFS, t=TILES)
        rows_out = hot_memory[:, 0:node_tiles * HROW].rearrange("p (t f) -> p t f", f=HROW)
        turned = sb("turned", [P, 2, 4, P])
        he = sb("he", [P, BUFS, TILES, HROW])
        z = sb("z", [P, TILES, G])
        same = sb("same", [P, 2, P])
        keep = sb("keep", [P, 2, P])
        run_fwd = sb("run_fwd", [P, P])
        run_max = sb("run_max", [P, P])
        ends = sb("ends", [P, 2, TILES])
        across = sb("across", [G, 2 * (TILES + 2)])
        start = sb("start", [P, 2, TILES])
        init = sb("init", [P, 2])
        shifted = sb("shifted", [P, P])
        weights_t = sb("weights_t", [P, P])
        drop = sb("drop", [G, 1])
        rescale = sb("rescale", [G, 1])
        rescale_diag = sb("rescale_diag", [G, G])
        msg = sb("msg", [P, TILES, G, GC])
        carry_in = sb("carry_in", [P, G, GC])
        carry_hot = sb("carry_hot", [P, 2, P])
        agg_sb = sb("agg_sb", [P, 2, G * GC])
        inv = sb("inv", [P, NGRP, G])
        back = xe[:, :, :, :].rearrange("p q t f -> p (q t f)")[:, 0:2 * NGRP * G * GC].rearrange(
            "p (b t g k) -> p b t g k", b=2, t=NGRP, g=G)
        normed = hot[:, :, :, :].rearrange("p q t f -> p (q t f)")[:, 0:NGRP * G * DH].rearrange(
            "p (t g k) -> p t g k", t=NGRP, g=G)

        turn_ps = [ps(f"turn_ps{i}") for i in range(2)]
        proj_ps = [ps(f"proj_ps{i}") for i in range(2)]
        scan_ps = ps("scan_ps")
        wt_ps = ps("wt_ps")
        agg_ps = [ps(f"agg_ps{i}") for i in range(2)]

        names = """weights_in attn_in x_first x_rest marks_in ident_zero ident_done iota_done consts_done zero_done
            w_turned w_ready w_step var_ready std_ready normed_ready n_turned ht_ready n_proj 
            node_rows base_added table_out fill_out node_bn node_mv inv_ready marks_ready
            gathered turned_ready turned_out proj_ready he_ready hot_ready z_ready zt_ready ends_ready across_in across_ready
            start_ready shifted_ready drop_ready weights_ready rescale_ready diag_ready factors_ready wt_ready msg_den msg_ready agg_done
            agg_out chain carried sums_out read_back0 read_back1 final_step out_ready out_done""".split()
        S = {n: sem(n) for n in names}
        x_in = [sem(f"x_in{q}") for q in range(BUFS)]
        idx_in = [sem(f"idx_in{q}") for q in range(BUFS)]
        runs_in = [sem(f"runs_in{q}") for q in range(BUFS)]
        window_in = [sem(f"window_in{q}{s}") for q in range(BUFS) for s in range(2)]
        gather_sem = [sem(f"gather{k}") for k in range(GSEM)]

        def wait(eng, s, value):
            if not isinstance(value, int) or value > 0:
                eng.wait_ge(s, value)

        def over(eng, count, unroll, body):
            whole = (count - 1) // unroll - 1
            for c in range(unroll):
                body(c, 0, c)
            with eng.Fori(1, whole) as i:
                for q in range(unroll):
                    body(unroll * i + q, i, q)
            for c in range(unroll * whole, count):
                body(c, c // unroll, c % unroll)

        def ahead(c, i, q, by):
            if isinstance(c, int) and c + by >= chunks:
                return None
            return c + by, i + (q + by) // BUFS, (q + by) % BUFS

        def bc(ap, axis, n):
            a = ap.unsqueeze(axis)
            shape = list(a.shape)
            shape[axis] = n
            return a.to_broadcast(shape)

        block = ctx.enter_context(nc.Block())

        @block.sync
        def _(sp):
            def hold(s, value):
                wait(sp, s, value)
                sp.nop(nofuse=True)

            x_tiles = x.rearrange("(t p) f -> p t f", p=P)
            for k, w in enumerate((w_src, w_dst, w_edge)):
                sp.dma_start(w_in[:, k, :], w).then_inc(S["weights_in"], 16)
            sp.dma_start(xn[:, 0:NGRP, :], x_tiles[:, 0:NGRP, :]).then_inc(S["x_first"], 16)
            sp.dma_start(xn[:, NGRP:node_tiles, :], x_tiles[:, NGRP:node_tiles, :]).then_inc(S["x_rest"], 16)

            def load(c, i, q):
                sp.dma_start(idx[:, q, :], src_t[:, bass.ds(c * TILES, TILES)]).then_inc(idx_in[q], 16)
                sp.dma_start(xe[:, q, :, :], edge[bass.ds(c, 1), :, :].rearrange("a p (t f) -> (a p) t f", t=TILES)
                             ).then_inc(x_in[q], 16)
                sp.dma_start(runs[:, q, :, :], dst_runs[bass.ds(c, 1), :, :].rearrange("a p (k e) -> (a p) k e", k=3)
                             ).then_inc(runs_in[q], 16)

            def load_windows(c, i, q):
                for s in range(2):
                    first = sp.value_load(hm_i[0:1, 0, bass.ds(2 * c + s, 1)], min_val=0, max_val=nodes)
                    sp.dma_start(window[:, q, s, :], edst[bass.ds(first, P), :]).then_inc(window_in[2 * q + s], 16)

            for c in range(BUFS):
                load(c, 0, c)
            table_tiles = table.rearrange("(t p) f -> p t f", p=P)
            edst_tiles = edst.rearrange("(t p) f -> p t f", p=P)

            def store_rows(g, _i, _q):
                hold(S["node_rows"], (g + 1) * NGRP)
                part = bass.ds(g * NGRP, NGRP)
                sp.dma_start(table_tiles[:, part, :], rows_out[:, part, 0:ROW]).then_inc(S["table_out"], 16)
                sp.dma_start(edst_tiles[:, part, :], rows_out[:, part, ROW:HROW]).then_inc(S["table_out"], 16)

            sp.wait_ge(S["zero_done"], 1)
            sp.dma_start(edst_tiles[:, node_tiles, :], zeros[:, 0:HEADS]).then_inc(S["table_out"], 16)
            over(sp, groups, 2, store_rows)
            sp.wait_ge(S["table_out"], 16 * table_stores)
            sp.wait_ge(S["marks_in"], 16 * 8)
            for c in range(BUFS):
                load_windows(c, 0, c)
            sp.wait_ge(S["fill_out"], 16)

            def store_windows(d):
                for s in range(2):
                    u = 2 * d + s
                    first = sp.value_load(hm_i[0:1, 0, bass.ds(u, 1)], min_val=0, max_val=nodes)
                    hold(S["agg_out"], u + 1)
                    hold(S["sums_out"], u * 16)
                    sp.dma_start(sums[bass.ds(first, P), :], agg_sb[:, s, :]).then_inc(S["sums_out"], 16)

            def step(c, i, q):
                if isinstance(c, int) and c == 0:
                    return
                after = ahead(c, i, q, 2)
                if after:
                    hold(S["z_ready"], c)
                    hold(S["gathered"], c)
                    hold(S["proj_ready"], c * pairs)
                    load(*after)
                    load_windows(*after)
                if not (isinstance(c, int) and c < 2):
                    store_windows(c - 2)

            over(sp, chunks, BUFS, step)
            store_windows(chunks - 2)
            store_windows(chunks - 1)
            sums_tiles = sums.rearrange("(t p) (g k) -> p t g k", p=P, k=GC)
            out_tiles = out.rearrange("(t p) f -> p t f", p=P)
            sp.wait_ge(S["sums_out"], 16 * halves)
            for g in range(groups + 1):
                if g < groups:
                    if g >= 2:
                        sp.wait_ge(S["final_step"], 3 * (g - 2) + 3)
                    sp.dma_start(back[:, g % 2, :, :, :].rearrange("p t g k -> p t (g k)"),
                                 sums_tiles[:, g * NGRP:(g + 1) * NGRP].rearrange("p t g k -> p t (g k)")
                                 ).then_inc(S[f"read_back{g % 2}"], 16)
                if g >= 1:
                    t0, t1 = (g - 1) * NGRP, g * NGRP
                    sp.wait_ge(S["out_ready"], g)
                    sp.dma_start(out_tiles[:, t0:t1, :], xn[:, t0:t1, :]).then_inc(S["out_done"], 16)
            sp.wait_ge(S["out_done"], 16 * groups)

        @block.gpsimd
        def _(g_):
            g_.memset(ident[:, :], 0.0).then_inc(S["ident_zero"], 1)
            g_.iota(iota_i[:, :], pattern=[[1, P]], base=0, channel_multiplier=0).then_inc(S["iota_done"], 1)
            g_.iota(iota_ci[:, :], pattern=[[0, 1]], base=0, channel_multiplier=1).then_inc(S["iota_done"], 1)
            g_.wait_ge(S["ident_zero"], 1)
            g_.affine_select(out=ident[:, :], in_=ident[:, :], compare_op=ALU.not_equal, fill=1.0, base=0,
                             pattern=[[-1, P]], channel_multiplier=1).then_inc(S["ident_done"], 1)
            g_.wait_ge(S["table_out"], 16 * table_stores)
            per = TILES // GSEM

            def confirm(c, t):
                g_.wait_ge(gather_sem[t % GSEM], 16 * (per * c + t // GSEM + 1))

            def step(c, i, q):
                g_.wait_ge(idx_in[q], 16 * (i + 1))
                wait(g_, S["msg_ready"], 2 * (c - BUFS + 1))
                for t in range(TILES):
                    if t >= LAG:
                        confirm(c, t - LAG)
                    elif not (isinstance(c, int) and c == 0):
                        confirm(c - 1, TILES - LAG + t)
                        if t == LAG - 1:
                            g_.sem_inc(S["gathered"], 1)
                    g_.nop(nofuse=True)
                    g_.indirect_dma_start(out=rows[:, q, t, :], out_offset=None, in_=table[:, :],
                                          in_offset=bass.IndirectOffsetOnAxis(ap=idx[:, q, t:t + 1], axis=0)
                                          ).then_inc(gather_sem[t % GSEM], 16)

            over(g_, chunks, BUFS, step)
            for t in range(TILES - LAG, TILES):
                confirm(chunks - 1, t)
            g_.sem_inc(S["gathered"], 1)

        @block.tensor
        def _(pe):
            pe.wait_ge(S["weights_in"], 48)
            pe.wait_ge(S["ident_done"], 1)
            pe.wait_ge(S["w_step"], 3)
            for k in range(3):
                pe.transpose(agg_ps[0][:, k * P:(k + 1) * P], w_in[:, k, :], ident[:, :])
            for k in range(3):
                last = pe.matmul(agg_ps[1][:, k * HEADS:(k + 1) * HEADS], w_in[:, k, :], a_diag[:, k, :],
                                 start=True, stop=True)
            last.then_inc(S["w_turned"], 1)

            def node_group(g, i, q):
                pe.wait_ge(S["normed_ready"], g + 1)
                for j in range(NGRP):
                    n = g * NGRP + j
                    b = (q * NGRP + j) % 2
                    wait(pe, S["ht_ready"], n - 1)
                    pe.transpose(turn_ps[b][:, 0:P], normal[:, q, j, :], ident[:, :]).then_inc(S["n_turned"], 1)
                    if not (isinstance(g, int) and g == 0 and j == 0):
                        node_project(n - 1, 1 - b)

            def node_project(n, b):
                if isinstance(n, int) and n == 0:
                    pe.wait_ge(S["w_ready"], 1)
                pe.wait_ge(S["ht_ready"], n + 1)
                wait(pe, S["base_added"], n - 1)
                pe.matmul(proj_ps[b][:, 0:2 * ROW], ht[:, b, :], w_node[:, :], start=True, stop=True
                          ).then_inc(S["n_proj"], 1)

            over(pe, groups, 2, node_group)
            node_project(node_tiles - 1, (node_tiles - 1) % 2)

            def turn(c, i, q, m):
                wait(pe, S["turned_out"], c * quads + m - 1)
                pe.wait_ge(S["hot_ready"], 2 * c + m // (quads // 2) + 1)
                for j in range(4):
                    last = pe.transpose(turn_ps[m % 2][:, j * P:(j + 1) * P], hot[:, q, 4 * m + j, :], ident[:, :])
                last.then_inc(S["turned_ready"], 1)

            def project(c, i, q, n):
                m = n // 2
                pe.wait_ge(S["turned_out"], c * quads + m + 1)
                wait(pe, S["he_ready"], c * pairs + n - 1)
                if n == 0:
                    pe.wait_ge(x_in[q], 16 * (i + 1))
                if n % (pairs // 2) == 0:
                    pe.wait_ge(window_in[2 * q + n // (pairs // 2)], 16 * (i + 1))
                for j in range(2):
                    o = j * HROW
                    pe.matmul(proj_ps[n % 2][:, o:o + ROW], xe[:, q, 2 * n + j, :], w_edge_t[:, :], start=True, stop=True)
                    last = pe.matmul(proj_ps[n % 2][:, o + ROW:o + HROW], turned[:, m % 2, 2 * (n % 2) + j, :],
                                     window[:, q, n // (pairs // 2), :], start=True, stop=True)
                last.then_inc(S["proj_ready"], 1)

            def front(c, i, q):
                for m in range(quads):
                    turn(c, i, q, m)
                    if m:
                        project(c, i, q, 2 * m - 2)
                        project(c, i, q, 2 * m - 1)
                project(c, i, q, pairs - 2)
                project(c, i, q, pairs - 1)

            def turn_logits(d):
                pe.wait_ge(S["z_ready"], d + 1)
                pe.transpose(scan_ps[:, 0:P], z[:, :, :].rearrange("p t g -> p (t g)"), ident[:, :]
                             ).then_inc(S["zt_ready"], 1)

            def gather_ends(d):
                pe.wait_ge(S["ends_ready"], d + 1)
                pe.matmul(scan_ps[0:G, P:P + 2 * TILES], group_sel[:, :], ends[:, :, :].rearrange("p a t -> p (a t)"),
                          start=True, stop=True).then_inc(S["across_in"], 1)

            def spread_starts(d):
                pe.wait_ge(S["across_ready"], d + 1)
                pe.matmul(scan_ps[:, P + 2 * TILES:P + 4 * TILES], group_sel_t[:, :],
                          across[:, :].rearrange("g (a t) -> g a t", a=2)[:, :, 0:TILES],
                          start=True, stop=True).then_inc(S["start_ready"], 1)

            def turn_weights(d):
                pe.wait_ge(S["diag_ready"], d + 1)
                pe.matmul(scan_ps[:, P + 4 * TILES:P + 4 * TILES + G], ones8[:, :], rescale_diag[:, :], start=True,
                          stop=True).then_inc(S["factors_ready"], 1)
                pe.wait_ge(S["weights_ready"], d + 1)
                wait(pe, S["msg_den"], 2 * d)
                pe.transpose(wt_ps[:, 0:P], weights_t[:, :], ident[:, :]).then_inc(S["wt_ready"], 1)

            def aggregate(d, q, s, t0, t1):
                u = 2 * d + s
                if t0 == 0:
                    pe.wait_ge(S["msg_ready"], u + 1)
                    wait(pe, S["agg_out"], u - 1)
                for t in range(s * HALF + t0, s * HALF + t1):
                    pe.matmul(agg_ps[s][:, 0:G * GC], hot[:, q, t, :], msg[:, t, :, :].rearrange("p g k -> p (g k)"),
                              start=(t == s * HALF), stop=False)
                if t1 < HALF:
                    return
                pe.wait_ge(S["carried"], d + 1)
                if s == 0:
                    carry = carry_in[:, :, :].rearrange("p g k -> p (g k)")
                else:
                    pe.wait_ge(S["agg_out"], u)
                    carry = agg_sb[:, 0, :]
                pe.matmul(agg_ps[s][:, 0:G * GC], carry_hot[:, s, :], carry, start=False, stop=True
                          ).then_inc(S["agg_done"], 1)

            def step(c, i, q):
                def sums_of(s, t0, t1):
                    if not (isinstance(c, int) and c == 0):
                        aggregate(c - 1, (q - 1) % BUFS, s, t0, t1)

                turn_logits(c)
                sums_of(0, 0, 3)
                gather_ends(c)
                sums_of(0, 3, 5)
                spread_starts(c)
                sums_of(0, 5, HALF)
                turn_weights(c)
                sums_of(1, 0, HALF)
                if ahead(c, i, q, 1):
                    front(*ahead(c, i, q, 1))

            front(0, 0, 0)
            over(pe, chunks, BUFS, step)
            for s in range(2):
                aggregate(chunks - 1, (chunks - 1) % BUFS, s, 0, HALF)

        @block.scalar
        def _(act):
            for k, a in enumerate((a_src, a_dst, a_edge)):
                act.dma_start(a_in[:, k:k + 1], a.rearrange("h (d o) -> (h d) o", o=1)).then_inc(S["attn_in"], 16)
            act.dma_start(dst_sb[:, :], dst_t).then_inc(S["marks_in"], 16)
            for k in range(3):
                act.dma_start(hm_i[:, k, :], half_marks[k:k + 1, :].to_broadcast([P, halves])).then_inc(S["marks_in"], 16)
            for k in range(2):
                act.dma_start(tm_i[:, k, :], tile_marks[2 * k:2 * k + 1, :].to_broadcast([G, tiles])
                              ).then_inc(S["marks_in"], 16)
                act.dma_start(tm_j[:, k, :], tile_marks[2 * k + 1:2 * k + 2, :].to_broadcast([G, tiles])
                              ).then_inc(S["marks_in"], 16)
            act.wait_ge(S["zero_done"], 1)
            act.dma_start(sums.rearrange("(t p) f -> p t f", p=P), bc(zeros[:, :], 1, node_tiles + 1)
                          ).then_inc(S["fill_out"], 16)
            act.wait_ge(S["w_turned"], 1)
            act.activation(w_node[:, 0:P], agg_ps[0][:, 0:P], ACT.Copy)
            act.activation(w_node[:, HROW:HROW + P], agg_ps[0][:, P:2 * P], ACT.Copy)
            act.activation(w_edge_t[:, 0:P], agg_ps[0][:, 2 * P:3 * P], ACT.Copy)
            act.activation(w_node[:, P:HROW], agg_ps[1][:, 0:2 * HEADS], ACT.Copy)
            act.activation(w_edge_t[:, P:ROW], agg_ps[1][:, 2 * HEADS:3 * HEADS], ACT.Copy).then_inc(S["w_ready"], 1)

            def node_std(g, i, q):
                act.wait_ge(S["var_ready"], g + 1)
                act.activation(spread[:, q, 1, :], spread[:, q, 0, :], ACT.Sqrt).then_inc(S["std_ready"], 1)

            def node_group(g, i, q):
                for j in range(NGRP):
                    n = g * NGRP + j
                    b = (q * NGRP + j) % 2
                    act.wait_ge(S["n_turned"], n + 1)
                    wait(act, S["n_proj"], n - 1)
                    act.activation(ht[:, b, :], turn_ps[b][:, 0:P], ACT.Relu).then_inc(S["ht_ready"], 1)
                    if j == NGRP // 2 and not (isinstance(g, int) and g == groups - 1):
                        node_std(g + 1, i, 1 - q)
                    if not (isinstance(g, int) and g == 0 and j == 0):
                        node_row(n - 1, 1 - b)

            def node_row(n, b):
                act.wait_ge(S["n_proj"], n + 1)
                act.activation(rows_out[:, bass.ds(n, 1), :].rearrange("p a f -> p (a f)"), proj_ps[b][:, 0:HROW],
                               ACT.Copy).then_inc(S["node_rows"], 1)

            node_std(0, 0, 0)
            over(act, groups, 2, node_group)
            node_row(node_tiles - 1, (node_tiles - 1) % 2)

            def turned_copy(c, i, q, m):
                k = c * quads + m
                act.wait_ge(S["turned_ready"], k + 1)
                wait(act, S["proj_ready"], 2 * (k - 1))
                act.activation(turned[:, m % 2, :, :], turn_ps[m % 2][:, :].rearrange("p (a f) -> p a f", a=4), ACT.Copy
                               ).then_inc(S["turned_out"], 1)

            def he_copy(c, i, q, n):
                if n == 0:
                    wait(act, S["msg_ready"], 2 * (c - BUFS + 1))
                act.wait_ge(S["proj_ready"], c * pairs + n + 1)
                act.activation(he[:, q, 2 * n:2 * n + 2, :],
                               proj_ps[n % 2][:, 0:2 * HROW].rearrange("p (a f) -> p a f", a=2), ACT.Copy
                               ).then_inc(S["he_ready"], 1)

            def front(c, i, q):
                for m in range(quads):
                    turned_copy(c, i, q, m)
                    if m:
                        he_copy(c, i, q, 2 * m - 2)
                        he_copy(c, i, q, 2 * m - 1)
                he_copy(c, i, q, pairs - 2)
                he_copy(c, i, q, pairs - 1)

            def exps(d):
                act.wait_ge(S["drop_ready"], d + 1)
                wait(act, S["diag_ready"], d)
                act.activation(rescale[:, :], drop[:, :], ACT.Exp).then_inc(S["rescale_ready"], 1)
                act.wait_ge(S["shifted_ready"], d + 1)
                wait(act, S["wt_ready"], d)
                act.activation(weights_t[:, :], shifted[:, :], ACT.Exp).then_inc(S["weights_ready"], 1)

            def put_weights(d, s):
                act.wait_ge(S["wt_ready"], d + 1)
                wait(act, S["agg_done"], 2 * d - 1 + s)
                a, b = s * HALF, (s + 1) * HALF
                act.activation(msg[:, a:b, :, DH:GC].rearrange("p t g o -> p (t g) o"),
                               wt_ps[:, a * G:b * G].rearrange("p (a o) -> p a o", o=1), ACT.Copy
                               ).then_inc(S["msg_den"], 1)

            def window_out(d, s):
                u = 2 * d + s
                act.wait_ge(S["agg_done"], u + 1)
                wait(act, S["sums_out"], 16 * (u - 1))
                if s == 1:
                    act.wait_ge(S["carried"], d + 1)
                act.activation(agg_sb[:, s, :], agg_ps[s][:, 0:G * GC], ACT.Copy).then_inc(S["agg_out"], 1)

            def step(c, i, q):
                exps(c)
                for s in range(2):
                    if not (isinstance(c, int) and c == 0):
                        window_out(c - 1, s)
                    put_weights(c, s)
                if ahead(c, i, q, 1):
                    front(*ahead(c, i, q, 1))

            front(0, 0, 0)
            over(act, chunks, BUFS, step)
            for s in range(2):
                window_out(chunks - 1, s)

        @block.vector
        def _(v):
            v.memset(zeros[:, :], 0.0).then_inc(S["zero_done"], 1)
            v.memset(carry_hot[:, :, :], 0.0).then_inc(S["consts_done"], 1)
            v.memset(agg_sb[:, 1, :], 0.0).then_inc(S["consts_done"], 1)
            v.memset(ones8[:, :], 1.0).then_inc(S["consts_done"], 1)
            v.memset(across[:, :], -BIG).then_inc(S["consts_done"], 1)
            v.memset(head_mask[:, :], 0.0).then_inc(S["w_step"], 1)
            v.wait_ge(S["w_step"], 1)
            for h in range(HEADS):
                last = v.memset(head_mask[h * DH:(h + 1) * DH, h:h + 1], 1.0)
            last.then_inc(S["w_step"], 1)
            v.wait_ge(S["w_step"], 2)
            v.wait_ge(S["attn_in"], 48)
            v.tensor_tensor(a_diag[:, :, :], bc(head_mask[:, :], 1, 3), bc(a_in[:, :], 2, HEADS), ALU.mult
                            ).then_inc(S["w_step"], 1)
            v.wait_ge(S["iota_done"], 2)
            v.tensor_copy(iota_row[:, :], iota_i[:, :]).then_inc(S["consts_done"], 1)
            v.tensor_copy(iota_col[:, :], iota_ci[:, :]).then_inc(S["consts_done"], 1)
            v.wait_ge(S["ident_done"], 1)
            v.tensor_reduce(tile_mask[:, :], ident[:, :].rearrange("p (t g) -> p t g", g=G), AX.X, ALU.add
                            ).then_inc(S["consts_done"], 1)
            v.tensor_reduce(group_sel[:, :], ident[:, :].rearrange("p (t g) -> p g t", g=G), AX.X, ALU.add
                            ).then_inc(S["consts_done"], 1)
            v.tensor_copy(group_sel_t[:, :].rearrange("c (t g) -> c t g", g=G), bc(ident[0:G, 0:G], 1, TILES)
                          ).then_inc(S["consts_done"], 1)

            def node_stats(g, i, q):
                wait(v, S["std_ready"], g - 1)
                for j in range(NGRP):
                    v.bn_stats(bn[:, q, j, :], xn[:, bass.ds(g * NGRP + j, 1), :].rearrange("p a f -> p (a f)")
                               ).then_inc(S["node_bn"], 1)
                for j in range(NGRP):
                    v.wait_ge(S["node_bn"], g * NGRP + j + 1)
                    v.bn_aggr(moments[:, q, j, :], bn[:, q, j, :]).then_inc(S["node_mv"], 1)
                v.wait_ge(S["node_mv"], (g + 1) * NGRP)
                v.tensor_scalar(spread[:, q, 0, :], moments[:, q, :, 1], EPS, None, ALU.add).then_inc(S["var_ready"], 1)

            def node_group(g, i, q):
                if not (isinstance(g, int) and g == groups - 1):
                    node_stats(g + 1, i, 1 - q)
                v.wait_ge(S["std_ready"], g + 1)
                v.reciprocal(spread[:, q, 2, :], spread[:, q, 1, :]).then_inc(S["inv_ready"], 1)
                v.wait_ge(S["inv_ready"], g + 1)
                wait(v, S["n_turned"], (g - 1) * NGRP)
                for j in range(NGRP):
                    last = v.tensor_scalar(normal[:, q, j, :], xn[:, bass.ds(g * NGRP + j, 1), :].rearrange("p a f -> p (a f)"),
                                           moments[:, q, j, 0:1], spread[:, q, 2, j:j + 1], ALU.subtract, ALU.mult)
                last.then_inc(S["normed_ready"], 1)
                if not (isinstance(g, int) and g == 0):
                    node_base(g - 1, 1 - q)

            def node_base(g, q):
                for j in range(NGRP):
                    n = g * NGRP + j
                    v.wait_ge(S["node_rows"], n + 1)
                    row = xn[:, bass.ds(n, 1), :].rearrange("p a f -> p (a f)")
                    v.tensor_tensor(row, row, proj_ps[(q * NGRP + j) % 2][:, HROW:2 * ROW], ALU.add
                                    ).then_inc(S["base_added"], 1)

            v.wait_ge(S["x_first"], 16)
            node_stats(0, 0, 0)
            v.wait_ge(S["x_rest"], 16)
            over(v, groups, 2, node_group)
            node_base(groups - 1, (groups - 1) % 2)

            v.wait_ge(S["marks_in"], 16 * 8)
            v.tensor_tensor(rel[:, :].rearrange("p (u t) -> p u t", t=HALF), dst_sb[:, :].rearrange("p (u t) -> p u t", t=HALF),
                            bc(hm_i[:, 0, :], 2, HALF), ALU.subtract).then_inc(S["marks_ready"], 1)
            v.wait_ge(S["consts_done"], 9)
            v.scalar_tensor_tensor(out=carry_sel[:, :], in0=hm_i[:, 2, :], scalar=iota_col[:, 0:1], in1=hm_i[:, 0, :],
                                   op0=ALU.add, op1=ALU.is_equal).then_inc(S["marks_ready"], 1)
            v.tensor_tensor(tile_keep[:, :, :], tm_i[:, :, :], tm_j[:, :, :], ALU.is_equal).then_inc(S["marks_ready"], 1)
            v.tensor_tensor(goes_on[:, :], hm_i[:, 1, :], hm_i[:, 0, :], ALU.is_equal).then_inc(S["marks_ready"], 1)
            v.wait_ge(S["marks_ready"], 4)
            v.tensor_tensor(carry_sel[:, :], carry_sel[:, :], goes_on[:, :], ALU.mult).then_inc(S["marks_ready"], 1)
            v.tensor_scalar(tile_keep[:, :, :], tile_keep[:, :, :], -0.5, 2 * BIG, ALU.add, ALU.mult
                            ).then_inc(S["marks_ready"], 1)
            v.wait_ge(S["marks_ready"], 6)

            def one_hot(c, i, q):
                for s in range(2):
                    wait(v, S["agg_done"], 2 * (c - BUFS + 1))
                    v.tensor_tensor(hot[:, q, s * HALF:(s + 1) * HALF, :], bc(iota_row[:, :], 1, HALF),
                                    bc(rel[:, bass.ds((2 * c + s) * HALF, HALF)], 2, P), ALU.is_equal
                                    ).then_inc(S["hot_ready"], 1)

            links = 10

            def softmax(d, i, q):
                done = [0]

                def link(ins):
                    done[0] += 1
                    ins.then_inc(S["chain"], 1)
                    v.wait_ge(S["chain"], d * links + done[0])

                v.wait_ge(runs_in[q], 16 * (i + 1))
                link(v.tensor_tensor(same[:, :, :], bc(runs[:, q, 0, :], 1, 2), runs[:, q, 1:3, :], ALU.is_equal))
                link(v.tensor_scalar(keep[:, :, :], same[:, :, :], -0.5, 2 * BIG, ALU.add, ALU.mult))
                v.wait_ge(S["he_ready"], (d + 1) * pairs)
                v.wait_ge(S["gathered"], d + 1)
                wait(v, S["zt_ready"], d)
                v.tensor_tensor(z[:, :, 0:HEADS], rows[:, q, :, P:ROW], he[:, q, :, ROW:HROW], ALU.add)
                link(v.tensor_tensor(z[:, :, HEADS:G], he[:, q, :, P:ROW], he[:, q, :, ROW:HROW], ALU.add))
                v.scalar_tensor_tensor(out=z[:, :, :], in0=z[:, :, :], scalar=SLOPE, in1=z[:, :, :],
                                       op0=ALU.mult, op1=ALU.max).then_inc(S["z_ready"], 1)
                v.wait_ge(S["zt_ready"], d + 1)
                logits = scan_ps[:, 0:P]
                link(v.tensor_tensor_scan(run_fwd[:, :], keep[:, 0, :], logits, -BIG, ALU.min, ALU.max))
                link(v.tensor_tensor_scan(run_max[:, ::-1], keep[:, 1, ::-1], run_fwd[:, ::-1], -BIG, ALU.min, ALU.max))
                v.tensor_scalar(ends[:, 0, :], tile_mask[:, :], run_fwd[:, P - 1:P], None, ALU.mult)
                v.tensor_scalar(ends[:, 1, :], tile_mask[:, :], run_max[:, 0:1], None, ALU.mult).then_inc(S["ends_ready"], 1)
                W = TILES + 2
                wait(v, S["start_ready"], d)
                link(v.tensor_copy(across[:, 0:1], across[:, TILES:TILES + 1]))
                v.wait_ge(S["across_in"], d + 1)
                v.tensor_tensor_scan(across[:, 1:TILES + 1], tile_keep[:, 0, bass.ds(d * TILES, TILES)],
                                     scan_ps[0:G, P:P + TILES], across[:, 0:1], ALU.min, ALU.max)
                v.tensor_tensor_scan(across[:, W - 1:W - 1 + TILES][:, ::-1],
                                     tile_keep[:, 1, bass.ds(d * TILES, TILES)],
                                     scan_ps[0:G, P + TILES:P + 2 * TILES][:, ::-1], -BIG, ALU.min, ALU.max
                                     ).then_inc(S["across_ready"], 1)
                v.wait_ge(S["start_ready"], d + 1)
                link(v.tensor_tensor(start[:, :, :],
                                     scan_ps[:, P + 2 * TILES:P + 4 * TILES].rearrange("p (a t) -> p a t", a=2),
                                     bc(tile_mask[:, :], 1, 2), ALU.mult))
                link(v.tensor_reduce(init[:, :], start[:, :, :], AX.X, ALU.add))
                link(v.tensor_tensor_scan(run_fwd[:, :], keep[:, 0, :], logits, init[:, 0:1], ALU.min, ALU.max))
                link(v.tensor_tensor_scan(run_max[:, ::-1], keep[:, 1, ::-1], run_fwd[:, ::-1], init[:, 1:2],
                                          ALU.min, ALU.max))
                wait(v, S["rescale_ready"], d)
                v.tensor_scalar(drop[:, :], across[:, 0:1], run_max[0:G, 0:1], 0.0, ALU.subtract, ALU.min
                                ).then_inc(S["drop_ready"], 1)
                wait(v, S["weights_ready"], d)
                v.tensor_tensor(shifted[:, :], logits, run_max[:, :], ALU.subtract).then_inc(S["shifted_ready"], 1)
                v.wait_ge(S["rescale_ready"], d + 1)
                wait(v, S["factors_ready"], d)
                v.tensor_scalar(rescale_diag[:, :], ident[0:G, 0:G], rescale[:, 0:1], None, ALU.mult
                                ).then_inc(S["diag_ready"], 1)
                for s in range(2):
                    v.wait_ge(S["msg_den"], 2 * d + s + 1)
                    a, b = s * HALF, (s + 1) * HALF
                    w = msg[:, a:b, :, DH:GC]
                    v.tensor_tensor(msg[:, a:b, 0:HEADS, 0:DH],
                                    rows[:, q, a:b, 0:P].rearrange("p t (h k) -> p t h k", k=DH),
                                    w[:, :, 0:HEADS, :].to_broadcast([P, HALF, HEADS, DH]), ALU.mult)
                    v.tensor_tensor(msg[:, a:b, HEADS:G, 0:DH],
                                    he[:, q, a:b, 0:P].rearrange("p t (h k) -> p t h k", k=DH),
                                    w[:, :, HEADS:G, :].to_broadcast([P, HALF, HEADS, DH]), ALU.mult
                                    ).then_inc(S["msg_ready"], 1)
                wait(v, S["agg_done"], 2 * d)
                wait(v, S["agg_out"], 2 * d)
                v.tensor_copy(carry_hot[:, :, 0], carry_sel[:, bass.ds(2 * d, 2)])
                v.wait_ge(S["factors_ready"], d + 1)
                v.tensor_tensor(carry_in[:, :, :], agg_sb[:, 1, :].rearrange("p (g k) -> p g k", k=GC),
                                bc(scan_ps[:, P + 4 * TILES:P + 4 * TILES + G], 2, GC), ALU.mult
                                ).then_inc(S["carried"], 1)
                assert done[0] == links, done[0]

            def step(c, i, q):
                softmax(c, i, q)
                if ahead(c, i, q, 2):
                    one_hot(*ahead(c, i, q, 2))

            v.wait_ge(S["table_out"], 16 * table_stores)
            one_hot(0, 0, 0)
            one_hot(1, 0, 1)
            over(v, chunks, BUFS, step)

            for g in range(groups):
                v.wait_ge(S[f"read_back{g % 2}"], 16 * (g // 2 + 1))
                v.tensor_scalar(inv[:, :, :], back[:, g % 2, :, :, DH], 0.5, None, ALU.max).then_inc(S["final_step"], 1)
                v.wait_ge(S["final_step"], 3 * g + 1)
                v.reciprocal(inv[:, :, :], inv[:, :, :]).then_inc(S["final_step"], 1)
                v.wait_ge(S["final_step"], 3 * g + 2)
                v.tensor_tensor(normed[:, :, :, :].rearrange("p t g k -> p (t g) k"),
                                back[:, g % 2, :, :, 0:DH].rearrange("p t g k -> p (t g) k"),
                                bc(inv[:, :, :].rearrange("p t g -> p (t g)"), 2, DH), ALU.mult).then_inc(S["final_step"], 1)
                v.wait_ge(S["final_step"], 3 * g + 3)
                rows_g = xn[:, g * NGRP:(g + 1) * NGRP, :]
                halves_n = normed[:, :, :, :].rearrange("p t (b h) k -> p t b (h k)", b=2)
                v.tensor_tensor(rows_g, rows_g, halves_n[:, :, 0, :], ALU.add).then_inc(S["base_added"], 1)
                v.wait_ge(S["base_added"], node_tiles + g + 1)
                v.tensor_tensor(rows_g, rows_g, halves_n[:, :, 1, :], ALU.add).then_inc(S["out_ready"], 1)


def kernel(**inputs):
    import numpy as np
    import concourse.bacc as bacc
    from concourse.bass_utils import run_bass_kernel_spmd

    a = {k: np.asarray(v) for k, v in inputs.items()}
    n, e = a["x"].shape[0], a["src"].shape[0]
    node_rows = -(-n // (P * NGRP)) * P * NGRP
    chunks = -(-e // CHUNK)
    edges = chunks * CHUNK
    x = np.zeros((node_rows, P), np.float32)
    x[:n] = a["x"]
    src = np.zeros(edges, np.int32)
    src[:e] = a["src"]
    dst = np.full(edges + 2, n, np.int32)
    dst[0] = -1
    dst[1:e + 1] = a["dst"]
    dst[edges + 1] = -1
    here, before, after = dst[1:-1], dst[:-2], dst[2:]
    edge = np.zeros((edges, P), np.float32)
    edge[:e] = a["edge_attr_128"]
    edge = np.ascontiguousarray(edge.reshape(chunks, CHUNK, P).transpose(0, 2, 1))
    runs = np.stack([here, before, after], 0).reshape(3, chunks, TILES, 1, P)
    runs = np.ascontiguousarray(np.broadcast_to(runs, (3, chunks, TILES, G, P)).transpose(1, 2, 3, 0, 4))
    step = HALF * P
    first = here[::step]
    none = np.full(1, -1, np.int32)
    half_marks = np.stack([first, before[::step], np.concatenate([none, first[:-1]])])
    t_first, t_last = here[::P], here[P - 1::P]
    turn_back = lambda m: m.reshape(chunks, TILES)[:, ::-1].reshape(-1)
    tile_marks = np.stack([t_last, np.concatenate([none, t_last[:-1]]),
                           turn_back(t_first), turn_back(np.concatenate([t_first[1:], none]))])
    arrays = {
        "x": x, "src_t": np.ascontiguousarray(src.reshape(-1, P).T), "dst_t": np.ascontiguousarray(here.reshape(-1, P).T),
        "dst_runs": runs.reshape(chunks, P, 3 * P), "half_marks": np.ascontiguousarray(half_marks),
        "tile_marks": np.ascontiguousarray(tile_marks), "edge": edge,
        "w_src": a["L0_gnn_W_src"], "w_dst": a["L0_gnn_W_dst"], "w_edge": a["L0_gnn_W_edge"],
        "a_src": a["L0_gnn_attn_src"], "a_dst": a["L0_gnn_attn_dst"], "a_edge": a["L0_gnn_attn_edge"],
    }
    nc = bacc.Bacc("TRN2", target_bir_lowering=False, num_devices=1)
    aps = [nc.dram_tensor(k, v.shape, mybir.dt.from_np(v.dtype), kind="ExternalInput").ap() for k, v in arrays.items()]
    out = nc.dram_tensor("out", (node_rows, P), F32, kind="ExternalOutput").ap()
    gnn_program(nc, *aps, out, n)
    got = run_bass_kernel_spmd(nc, [arrays], core_ids=[0])
    return got.results[0]["out"][:n]
```

```python
from contextlib import ExitStack

import concourse.bass as bass
from concourse import mybir

F32 = mybir.dt.float32
BF16 = mybir.dt.bfloat16
I32 = mybir.dt.int32
ALU = mybir.AluOpType
ACT = mybir.ActivationFunctionType
AX = mybir.AxisListType

P = 128
HEADS = 4
DH = 32
G = 2 * HEADS
GC = DH + 1
ROW = P + HEADS
NROW = ROW + HEADS
PARTS = 3
HROW = ROW + PARTS * HEADS
TILES = 16
HALF = TILES // 2
CHUNK = TILES * P
BIG = 1.0e30
EPS = 1e-5
SLOPE = 0.2
NGRP = 7
PACK = 512 // HROW
BUFS = 3
LAG = 8


def gnn_program(nc, x, src_t, dst_t, dst_runs, half_marks, tile_marks, dst_line, edge, w_src, w_dst, w_edge,
                a_src, a_dst, a_edge, out, nodes):
    node_tiles = x.shape[0] // P
    groups = node_tiles // NGRP
    chunks = edge.shape[0]
    tiles = chunks * TILES
    halves = 2 * chunks
    quads = TILES // 4
    packs = [range(t, min(t + PACK, TILES)) for t in range(0, TILES, PACK)]
    wide = (node_tiles + 1) * P
    assert groups * NGRP == node_tiles and groups >= 4 and chunks >= 3 * BUFS

    table = nc.dram_tensor("table", (node_tiles * P, ROW), F32, kind="Internal").ap()
    edst = nc.dram_tensor("edst", (wide, PARTS * HEADS), BF16, kind="Internal").ap()
    sums = nc.dram_tensor("sums", (wide, G * GC), F32, kind="Internal").ap()
    base = nc.dram_tensor("base", (wide, P), F32, kind="Internal").ap()
    peaks = nc.dram_tensor("peaks", (wide, G), F32, kind="Internal").ap()

    ctx = ExitStack()
    with ctx:
        def sb(name, shape, dt=F32):
            return ctx.enter_context(nc.sbuf_tensor(name, shape, dt))

        def ps(name):
            return ctx.enter_context(nc.psum_tensor(name, [P, 512], F32))

        def sem(name):
            return ctx.enter_context(nc.semaphore(name))

        ident = sb("ident", [P, P])
        iota_row = sb("iota_row", [P, P])
        iota_i = sb("iota_i", [P, P], I32)
        iota_col = sb("iota_col", [P, 1])
        iota_ci = sb("iota_ci", [P, 1], I32)
        ones8 = sb("ones8", [G, P])
        tile_mask = sb("tile_mask", [P, TILES])
        group_sel = sb("group_sel", [P, G])
        group_sel_t = sb("group_sel_t", [G, P])
        w_in = sb("w_in", [P, 3, P])
        a_in = sb("a_in", [P, 3])
        head_mask = sb("head_mask", [P, HEADS])
        a_diag = sb("a_diag", [P, 3, HEADS])
        w_node = sb("w_node", [P, 2 * ROW])
        w_edge_t = sb("w_edge_t", [P, ROW])
        xn = sb("xn", [P, node_tiles, P])
        normal = sb("normal", [P, 2, NGRP, P])
        bn = sb("bn", [P, 2, NGRP, 6])
        moments = sb("moments", [P, 2, NGRP, 2])
        spread = sb("spread", [P, 2, 3, NGRP])
        ht = sb("ht", [P, 2, P])
        edst_parts = sb("edst_parts", [P, node_tiles + 1, PARTS, HEADS], BF16)
        edst_rest = sb("edst_rest", [P, 2, NGRP, HEADS])
        zeros = sb("zeros", [P, G * GC])
        dst_sb = sb("dst_sb", [P, tiles], I32)
        rel = sb("rel", [P, tiles])
        hm_i = sb("hm_i", [P, 3, halves], I32)
        carry_sel = sb("carry_sel", [P, halves])
        goes_on = sb("goes_on", [P, halves])
        tile_keep = sb("tile_keep", [G, 2, tiles])
        idx = sb("idx", [P, BUFS, TILES], I32)
        rows = sb("rows", [P, BUFS, TILES, ROW])
        xe = sb("xe", [P, BUFS, TILES, P])
        runs = sb("runs", [P, BUFS, 3, P], I32)
        window = sb("window", [P, BUFS, 2, PARTS * HEADS], BF16)
        hot_memory = sb("hot_memory", [P, max(BUFS * TILES * P, node_tiles * NROW)])
        hot = hot_memory[:, 0:BUFS * TILES * P].rearrange("p (q t f) -> p q t f", q=BUFS, t=TILES)
        rows_out = hot_memory[:, 0:node_tiles * NROW].rearrange("p (t f) -> p t f", f=NROW)
        turned = sb("turned", [P, TILES, P], BF16)
        he = sb("he", [P, BUFS, TILES, HROW])
        edst_edge = sb("edst_edge", [P, TILES, HEADS])
        z = sb("z", [P, TILES, G])
        same = sb("same", [P, 2, P])
        keep = sb("keep", [P, 2, P])
        run_fwd = sb("run_fwd", [P, P])
        run_max = sb("run_max", [P, P])
        ends = sb("ends", [P, 2, TILES])
        across = sb("across", [G, 2 * (TILES + 2)])
        start = sb("start", [P, 2, TILES])
        init = sb("init", [P, 2])
        shifted = sb("shifted", [P, P])
        weights_t = sb("weights_t", [P, P])
        drop = sb("drop", [G, 1])
        rescale = sb("rescale", [G, 1])
        rescale_diag = sb("rescale_diag", [G, G])
        msg = sb("msg", [P, TILES, G, GC])
        carry_in = sb("carry_in", [P, G, GC])
        carry_hot = sb("carry_hot", [P, 2, P])
        agg_sb = sb("agg_sb", [P, 2, G * GC])
        base_rows = sb("base_rows", [P, BUFS, 2, P])
        divisors = sb("divisors", [P, 2, G])
        shares = sb("shares", [P, 2, G, DH])
        result = sb("result", [P, 2, P])
        msg_memory = msg[:, :, :, :].rearrange("p t g k -> p (t g k)")
        tm_i, tm_j = (msg_memory[0:G, k * 2 * tiles:(k + 1) * 2 * tiles].bitcast(I32).rearrange("g (a t) -> g a t", a=2)
                      for k in range(2))
        he_memory = he[:, :, :, :].rearrange("p q t f -> p (q t f)")
        h_dst = he_memory[:, 1024:1024 + 2 * NGRP * P].rearrange("p (q j f) -> p q j f", q=2, j=NGRP)
        line = he_memory[:, 0:tiles + 1].bitcast(I32)
        line_steps = msg_memory[:, 4 * tiles:5 * tiles]
        extremes = sb("extremes", [P, 3])
        unfit = sb("unfit", [P, 1])
        any_order = sb("any_order", [1, 1], I32)
        src_one = idx[:, 0, 0:1]
        dst_one = idx[:, 1, 0:1]
        src_all = he_memory[:, 0:tiles].bitcast(I32)
        x_one = xe[:, 0, 0, :]
        rows_one = rows[:, 0, 0, :]
        edst_one = window[:, 0, 0, :]
        no_peak = sb("no_peak", [P, G])
        dst_f = sb("dst_f", [P, 1])
        peers = hot[:, 0, 0, :]
        cap = hot[:, 0, 1, :]
        z_one = z[:, 0, :]
        z_wide = hot[0:G, 1, 0:G, :]
        capped = hot[:, 2, 0:G, :]
        peak_old = sb("peak_old", [P, G])
        peak_new = sb("peak_new", [P, G])
        below = sb("below", [P, 2, G])
        sums_old = agg_sb[:, 0, :]
        sums_new = agg_sb[:, 1, :]
        msg_one = msg[:, 0, :, :]
        inv = sb("inv", [P, NGRP, G])
        back = xe[:, :, :, :].rearrange("p q t f -> p (q t f)")[:, 0:2 * NGRP * G * GC].rearrange(
            "p (b t g k) -> p b t g k", b=2, t=NGRP, g=G)
        normed = hot[:, :, :, :].rearrange("p q t f -> p (q t f)")[:, 0:NGRP * G * DH].rearrange(
            "p (t g k) -> p t g k", t=NGRP, g=G)

        turn_ps = [ps(f"turn_ps{i}") for i in range(2)]
        proj_ps = [ps(f"proj_ps{i}") for i in range(2)]
        scan_ps = ps("scan_ps")
        wt_ps = ps("wt_ps")
        agg_ps = [ps(f"agg_ps{i}") for i in range(2)]

        names = """weights_in attn_in x_first x_second x_rest marks_in
            ident_zero ident_done iota_done consts_done zero_done w_turned w_ready w_step
            node_bn node_mv var_ready std_ready inv_ready normed_ready n_turned ht_ready n_proj node_rows
            split split_ready base_added table_out edst_out base_out fill_out
            marks_ready line_step unfit_ready order_turned order_known
            hot_ready turned_ready turned_out proj_ready he_ready same_ready keep_ready chain
            z_ready zt_ready ends_ready across_in across_ready start_ready shifted_ready drop_ready
            weights_ready rescale_ready diag_ready factors_ready wt_ready msg_den msg_ready
            agg_done agg_out carried final_link half_result result_ready windows_out
            any_fill any_in any_ids any_fetched any_turned any_z any_zt any_spread any_logits any_below any_exps
            any_msg any_agg any_new any_put any_step
            read_back0 read_back1 final_step sum_added out_ready out_done""".split()
        S = {n: sem(n) for n in names}
        x_in = [sem(f"x_in{q}") for q in range(BUFS)]
        idx_in = [sem(f"idx_in{q}") for q in range(BUFS)]
        runs_in = [sem(f"runs_in{q}") for q in range(BUFS)]
        base_in = [sem(f"base_in{q}") for q in range(BUFS)]
        window_in = [sem(f"window_in{q}{s}") for q in range(BUFS) for s in range(2)]
        gather_sem = [sem(f"gather{k}") for k in range(TILES)]

        def wait(eng, s, value):
            if not isinstance(value, int) or value > 0:
                eng.wait_ge(s, value)

        def over(eng, count, unroll, body):
            whole = (count - 1) // unroll - 1
            for c in range(unroll):
                body(c, 0, c)
            with eng.Fori(1, whole) as i:
                for q in range(unroll):
                    body(unroll * i + q, i, q)
            for c in range(unroll * whole, count):
                body(c, c // unroll, c % unroll)

        def ahead(c, i, q, by):
            if isinstance(c, int) and c + by >= chunks:
                return None
            return c + by, i + (q + by) // BUFS, (q + by) % BUFS

        def bc(ap, axis, n):
            a = ap.unsqueeze(axis)
            shape = list(a.shape)
            shape[axis] = n
            return a.to_broadcast(shape)

        block = ctx.enter_context(nc.Block())

        @block.sync
        def _(sp):
            def hold(s, value):
                wait(sp, s, value)
                sp.nop(nofuse=True)

            x_tiles = x.rearrange("(t p) f -> p t f", p=P)
            sp.dma_start(xn[:, 0:NGRP, :], x_tiles[:, 0:NGRP, :]).then_inc(S["x_first"], 16)
            for k, w in enumerate((w_src, w_dst, w_edge)):
                sp.dma_start(w_in[:, k, :], w).then_inc(S["weights_in"], 16)
            sp.dma_start(xn[:, NGRP:2 * NGRP, :], x_tiles[:, NGRP:2 * NGRP, :]).then_inc(S["x_second"], 16)
            sp.dma_start(xn[:, 2 * NGRP:node_tiles, :], x_tiles[:, 2 * NGRP:node_tiles, :]).then_inc(S["x_rest"], 16)

            def load(c, i, q):
                sp.dma_start(idx[:, q, :], src_t[:, bass.ds(c * TILES, TILES)]).then_inc(idx_in[q], 16)
                sp.dma_start(xe[:, q, :, :], edge[bass.ds(c, 1), :, :].rearrange("a p (t f) -> (a p) t f", t=TILES)
                             ).then_inc(x_in[q], 16)
                sp.dma_start(runs[:, q, :, :], dst_runs[bass.ds(c, 1), :, :].rearrange("a p (k e) -> (a p) k e", k=3)
                             ).then_inc(runs_in[q], 16)

            def load_windows(c, i, q):
                for s in range(2):
                    first = sp.value_load(hm_i[0:1, 0, bass.ds(2 * c + s, 1)], min_val=0, max_val=nodes)
                    sp.dma_start(window[:, q, s, :], edst[bass.ds(first, P), :]).then_inc(window_in[2 * q + s], 16)

            sp.dma_start(dst_sb[:, :], dst_t).then_inc(S["marks_in"], 16)
            sp.dma_start(line[:, :], dst_line).then_inc(S["marks_in"], 16)
            for k in range(3):
                sp.dma_start(hm_i[:, k, :], half_marks[k:k + 1, :].to_broadcast([P, halves])).then_inc(S["marks_in"], 16)
            for k in range(2):
                sp.dma_start(tm_i[:, k, :], tile_marks[2 * k:2 * k + 1, :].to_broadcast([G, tiles])
                             ).then_inc(S["marks_in"], 16)
                sp.dma_start(tm_j[:, k, :], tile_marks[2 * k + 1:2 * k + 2, :].to_broadcast([G, tiles])
                             ).then_inc(S["marks_in"], 16)

            def load_base(c, i, q):
                for s in range(2):
                    first = sp.value_load(hm_i[0:1, 0, bass.ds(2 * c + s, 1)], min_val=0, max_val=nodes)
                    sp.dma_start(base_rows[:, q, s, :], base[bass.ds(first, P), :]).then_inc(base_in[q], 16)

            for c in range(BUFS):
                load(c, 0, c)
            table_tiles = table.rearrange("(t p) f -> p t f", p=P)
            out_tiles = out.rearrange("(t p) f -> p t f", p=P)
            base_tiles = base.rearrange("(t p) f -> p t f", p=P)
            edst_tiles = edst.rearrange("(t p) f -> p t f", p=P)

            def store_base(g):
                hold(S["base_added"], g + 1)
                part = bass.ds(g * NGRP, NGRP)
                sp.dma_start(base_tiles[:, part, :], xn[:, part, :]).then_inc(S["base_out"], 16)
                sp.dma_start(out_tiles[:, part, :], xn[:, part, :]).then_inc(S["fill_out"], 16)

            def store_rows(g, _i, _q):
                hold(S["node_rows"], (g + 1) * NGRP)
                part = bass.ds(g * NGRP, NGRP)
                sp.dma_start(table_tiles[:, part, :], rows_out[:, part, 0:ROW]).then_inc(S["table_out"], 16)
                hold(S["split_ready"], g + 1)
                sp.dma_start(edst_tiles[:, part, :], edst_parts[:, part, :, :].rearrange("p t a h -> p t (a h)")
                             ).then_inc(S["edst_out"], 16)
                if not (isinstance(g, int) and g == 0):
                    store_base(g - 1)

            sp.wait_ge(S["zero_done"], 2)
            sp.dma_start(edst_tiles[:, node_tiles, :], edst_parts[:, node_tiles, :, :].rearrange("p a h -> p (a h)")
                         ).then_inc(S["edst_out"], 16)
            sp.dma_start(base_tiles[:, node_tiles, :], zeros[:, 0:P]).then_inc(S["base_out"], 16)
            sp.dma_start(out_tiles[:, node_tiles, :], zeros[:, 0:P]).then_inc(S["fill_out"], 16)
            over(sp, groups, 2, store_rows)
            sp.wait_ge(S["edst_out"], 16 * (groups + 1))
            sp.wait_ge(S["marks_in"], 16 * 9)
            for c in range(BUFS):
                load_windows(c, 0, c)
            store_base(groups - 1)
            sp.wait_ge(S["base_out"], 16 * (groups + 1))
            load_base(0, 0, 0)
            sp.wait_ge(S["fill_out"], 16 * (groups + 1))

            def store_windows(d):
                hold(S["result_ready"], d + 1)
                for s in range(2):
                    u = 2 * d + s
                    first = sp.value_load(hm_i[0:1, 0, bass.ds(u, 1)], min_val=0, max_val=nodes)
                    hold(S["windows_out"], u * 16)
                    sp.dma_start(out[bass.ds(first, P), :], result[:, s, :]).then_inc(S["windows_out"], 16)

            def step(c, i, q):
                if isinstance(c, int) and c == 0:
                    return
                after = ahead(c, i, q, 2)
                if after:
                    hold(S["z_ready"], c)
                    hold(S["proj_ready"], c * len(packs))
                    load(*after)
                    load_windows(*after)
                hold(S["result_ready"], c - 2)
                load_base(c, i, q)
                if not (isinstance(c, int) and c < 2):
                    store_windows(c - 2)

            over(sp, chunks, BUFS, step)
            store_windows(chunks - 2)
            store_windows(chunks - 1)
            sp.wait_ge(S["windows_out"], 16 * halves)
            sp.wait_ge(S["order_known"], 1)
            with sp.If(sp.value_load(any_order[0:1, 0:1], min_val=0, max_val=1) > 0):
                sp.dma_start(sums.rearrange("(t p) f -> p t f", p=P), bc(zeros[:, :], 1, node_tiles + 1)
                             ).then_inc(S["any_fill"], 16)
                sp.dma_start(peaks.rearrange("(t p) f -> p t f", p=P), bc(no_peak[:, :], 1, node_tiles + 1)
                             ).then_inc(S["any_fill"], 16)
                sp.dma_start(src_all, src_t).then_inc(S["any_fill"], 16)
                sp.wait_ge(S["any_fill"], 48)

                def any_chunk(c):
                    for k in range(TILES):
                        if not (isinstance(c, int) and c == 0 and k == 0):
                            hold(S["any_put"], 32 * (c * TILES + k))
                        sp.dma_start(x_one, edge[bass.ds(c, 1), :, k * P:(k + 1) * P].rearrange("a p f -> (a p) f")
                                     ).then_inc(S["any_in"], 16)

                any_chunk(0)
                with sp.Fori(1, chunks) as c:
                    any_chunk(c)
                sp.wait_ge(S["any_put"], 32 * tiles)
                sums_tiles = sums.rearrange("(t p) (g k) -> p t g k", p=P, k=GC)
                for g in range(groups + 1):
                    if g < groups:
                        if g >= 2:
                            sp.wait_ge(S["final_step"], 3 * (g - 2) + 3)
                        sp.dma_start(back[:, g % 2, :, :, :].rearrange("p t g k -> p t (g k)"),
                                     sums_tiles[:, g * NGRP:(g + 1) * NGRP].rearrange("p t g k -> p t (g k)")
                                     ).then_inc(S[f"read_back{g % 2}"], 16)
                    if g >= 1:
                        t0, t1 = (g - 1) * NGRP, g * NGRP
                        sp.wait_ge(S["out_ready"], g)
                        sp.dma_start(out_tiles[:, t0:t1, :], xn[:, t0:t1, :]).then_inc(S["out_done"], 16)
                sp.wait_ge(S["out_done"], 16 * groups)

        @block.gpsimd
        def _(g_):
            g_.memset(ident[:, :], 0.0).then_inc(S["ident_zero"], 1)
            g_.iota(iota_i[:, :], pattern=[[1, P]], base=0, channel_multiplier=0).then_inc(S["iota_done"], 1)
            g_.iota(iota_ci[:, :], pattern=[[0, 1]], base=0, channel_multiplier=1).then_inc(S["iota_done"], 1)
            g_.wait_ge(S["ident_zero"], 1)
            g_.affine_select(out=ident[:, :], in_=ident[:, :], compare_op=ALU.not_equal, fill=1.0, base=0,
                             pattern=[[-1, P]], channel_multiplier=1).then_inc(S["ident_done"], 1)

            nsplit = 2 * (PARTS - 1)

            def node_split(g, i, q):
                g_.wait_ge(S["node_rows"], (g + 1) * NGRP)
                part = bass.ds(g * NGRP, NGRP)
                left = rows_out[:, part, ROW:NROW]
                for k in range(PARTS):
                    g_.tensor_copy(edst_parts[:, part, k, :], left
                                   ).then_inc(S["split" if k < PARTS - 1 else "split_ready"], 1)
                    if k < PARTS - 1:
                        g_.wait_ge(S["split"], g * nsplit + 2 * k + 1)
                        g_.tensor_tensor(edst_rest[:, k, :, :], left, edst_parts[:, part, k, :], ALU.subtract
                                        ).then_inc(S["split"], 1)
                        g_.wait_ge(S["split"], g * nsplit + 2 * k + 2)
                        left = edst_rest[:, k, :, :]
                g_.tensor_tensor(xn[:, part, :], xn[:, part, :], h_dst[:, q, :, :], ALU.add).then_inc(S["base_added"], 1)

            over(g_, groups, 2, node_split)
            g_.wait_ge(S["table_out"], 16 * groups)

            def confirm(c, t):
                g_.wait_ge(gather_sem[t], 16 * (c + 1))

            def step(c, i, q):
                g_.wait_ge(idx_in[q], 16 * (i + 1))
                wait(g_, S["msg_ready"], 2 * (c - BUFS + 1))
                for t in range(TILES):
                    if t >= LAG:
                        confirm(c, t - LAG)
                    elif not (isinstance(c, int) and c == 0):
                        confirm(c - 1, TILES - LAG + t)
                    g_.nop(nofuse=True)
                    g_.indirect_dma_start(out=rows[:, q, t, :], out_offset=None, in_=table[:, :],
                                          in_offset=bass.IndirectOffsetOnAxis(ap=idx[:, q, t:t + 1], axis=0)
                                          ).then_inc(gather_sem[t], 16)

            over(g_, chunks, BUFS, step)
            for t in range(TILES - LAG, TILES):
                confirm(chunks - 1, t)

            def any_tile(t):
                g_.wait_ge(S["any_ids"], 2 * (t + 1))
                g_.nop(nofuse=True)
                for one, held, by in ((rows_one, table, src_one), (edst_one, edst, dst_one),
                                      (peak_old[:, :], peaks, dst_one), (sums_old, sums, dst_one)):
                    g_.indirect_dma_start(out=one, out_offset=None, in_=held[:, :],
                                          in_offset=bass.IndirectOffsetOnAxis(ap=by, axis=0)
                                          ).then_inc(S["any_fetched"], 16)
                g_.wait_ge(S["any_new"], t + 1)
                g_.nop(nofuse=True)
                for one, held in ((peak_new[:, :], peaks), (sums_new, sums)):
                    g_.indirect_dma_start(out=held[:, :], out_offset=bass.IndirectOffsetOnAxis(ap=dst_one, axis=0),
                                          in_=one, in_offset=None).then_inc(S["any_put"], 16)

            g_.wait_ge(S["order_known"], 1)
            with g_.If(g_.value_load(any_order[0:1, 0:1], min_val=0, max_val=1) > 0):
                with g_.Fori(0, tiles) as t:
                    any_tile(t)

        @block.tensor
        def _(pe):
            pe.wait_ge(S["weights_in"], 48)
            pe.wait_ge(S["ident_done"], 1)
            pe.wait_ge(S["w_step"], 3)
            for k in range(3):
                pe.transpose(agg_ps[0][:, k * P:(k + 1) * P], w_in[:, k, :], ident[:, :])
            for k in range(3):
                last = pe.matmul(agg_ps[1][:, k * HEADS:(k + 1) * HEADS], w_in[:, k, :], a_diag[:, k, :],
                                 start=True, stop=True)
            last.then_inc(S["w_turned"], 1)

            def node_group(g, i, q):
                pe.wait_ge(S["normed_ready"], g + 1)
                for j in range(NGRP):
                    n = g * NGRP + j
                    b = (q * NGRP + j) % 2
                    wait(pe, S["ht_ready"], n - 1)
                    pe.transpose(turn_ps[b][:, 0:P], normal[:, q, j, :], ident[:, :]).then_inc(S["n_turned"], 1)
                    if not (isinstance(g, int) and g == 0 and j == 0):
                        node_project(n - 1, 1 - b)

            def node_project(n, b):
                if isinstance(n, int) and n == 0:
                    pe.wait_ge(S["w_ready"], 1)
                pe.wait_ge(S["ht_ready"], n + 1)
                wait(pe, S["node_rows"], n - 1)
                pe.matmul(proj_ps[b][:, 0:2 * ROW], ht[:, b, :], w_node[:, :], start=True, stop=True
                          ).then_inc(S["n_proj"], 1)

            over(pe, groups, 2, node_group)
            node_project(node_tiles - 1, (node_tiles - 1) % 2)

            def turn(c, i, q, m):
                wait(pe, S["turned_out"], c * quads + m - 1)
                pe.wait_ge(S["hot_ready"], 2 * c + m // (quads // 2) + 1)
                for j in range(4):
                    last = pe.transpose(turn_ps[m % 2][:, j * P:(j + 1) * P], hot[:, q, 4 * m + j, :], ident[:, :])
                last.then_inc(S["turned_ready"], 1)

            def project(c, i, q, n):
                pe.wait_ge(S["turned_out"], c * quads + packs[n][-1] // 4 + 1)
                wait(pe, S["he_ready"], c * len(packs) + n - 1)
                if n == 0:
                    pe.wait_ge(x_in[q], 16 * (i + 1))
                    for s in range(2):
                        pe.wait_ge(window_in[2 * q + s], 16 * (i + 1))
                for j, t in enumerate(packs[n]):
                    o = j * HROW
                    pe.matmul(proj_ps[n % 2][:, o:o + ROW], xe[:, q, t, :], w_edge_t[:, :], start=True, stop=True)
                    last = pe.matmul(proj_ps[n % 2][:, o + ROW:o + HROW], turned[:, t, :],
                                     window[:, q, t // HALF, :], start=True, stop=True)
                last.then_inc(S["proj_ready"], 1)

            def front_rest(c, i, q):
                for n in range(len(packs)):
                    project(c, i, q, n)
                    if n + 2 < quads:
                        turn(c, i, q, n + 2)

            def turn_logits(d):
                pe.wait_ge(S["z_ready"], d + 1)
                pe.transpose(scan_ps[:, 0:P], z[:, :, :].rearrange("p t g -> p (t g)"), ident[:, :]
                             ).then_inc(S["zt_ready"], 1)

            def gather_ends(d):
                pe.wait_ge(S["ends_ready"], d + 1)
                pe.matmul(scan_ps[0:G, P:P + 2 * TILES], group_sel[:, :], ends[:, :, :].rearrange("p a t -> p (a t)"),
                          start=True, stop=True).then_inc(S["across_in"], 1)

            def spread_starts(d):
                pe.wait_ge(S["across_ready"], d + 1)
                pe.matmul(scan_ps[:, P + 2 * TILES:P + 4 * TILES], group_sel_t[:, :],
                          across[:, :].rearrange("g (a t) -> g a t", a=2)[:, :, 0:TILES],
                          start=True, stop=True).then_inc(S["start_ready"], 1)

            def turn_weights(d):
                pe.wait_ge(S["diag_ready"], d + 1)
                pe.matmul(scan_ps[:, P + 4 * TILES:P + 4 * TILES + G], ones8[:, :], rescale_diag[:, :], start=True,
                          stop=True).then_inc(S["factors_ready"], 1)
                pe.wait_ge(S["weights_ready"], d + 1)
                wait(pe, S["msg_den"], 2 * d)
                pe.transpose(wt_ps[:, 0:P], weights_t[:, :], ident[:, :]).then_inc(S["wt_ready"], 1)

            def aggregate(d, q, s, t0, t1):
                u = 2 * d + s
                if t0 == 0:
                    pe.wait_ge(S["msg_ready"], u + 1)
                    wait(pe, S["agg_out"], u - 1)
                for t in range(s * HALF + t0, s * HALF + t1):
                    pe.matmul(agg_ps[s][:, 0:G * GC], hot[:, q, t, :], msg[:, t, :, :].rearrange("p g k -> p (g k)"),
                              start=(t == s * HALF), stop=False)
                if t1 < HALF:
                    return
                pe.wait_ge(S["carried"], d + 1)
                if s == 0:
                    carry = carry_in[:, :, :].rearrange("p g k -> p (g k)")
                else:
                    pe.wait_ge(S["agg_out"], u)
                    carry = agg_sb[:, 0, :]
                pe.matmul(agg_ps[s][:, 0:G * GC], carry_hot[:, s, :], carry, start=False, stop=True
                          ).then_inc(S["agg_done"], 1)

            def step(c, i, q):
                def sums_of(s, t0, t1):
                    if not (isinstance(c, int) and c == 0):
                        aggregate(c - 1, (q - 1) % BUFS, s, t0, t1)

                after = ahead(c, i, q, 1)
                sums_of(0, 0, 4)
                turn_logits(c)
                sums_of(0, 4, 6)
                gather_ends(c)
                sums_of(0, 6, HALF)
                if after:
                    turn(*after, 0)
                spread_starts(c)
                if after:
                    turn(*after, 1)
                sums_of(1, 0, HALF // 2)
                turn_weights(c)
                sums_of(1, HALF // 2, HALF)
                if after:
                    front_rest(*after)

            pe.wait_ge(S["unfit_ready"], 1)
            pe.matmul(wt_ps[0:1, 0:P], unfit[:, :], ident[:, :], start=True, stop=True).then_inc(S["order_turned"], 1)
            turn(0, 0, 0, 0)
            turn(0, 0, 0, 1)
            front_rest(0, 0, 0)
            over(pe, chunks, BUFS, step)
            for s in range(2):
                aggregate(chunks - 1, (chunks - 1) % BUFS, s, 0, HALF)

            def any_tile(t):
                pe.wait_ge(S["any_ids"], 2 * (t + 1))
                pe.matmul(turn_ps[0][:, 0:P], dst_f[:, 0:1].to_broadcast([P, P]), ident[:, :], start=True, stop=True)
                pe.matmul(proj_ps[0][:, 0:ROW], x_one, w_edge_t[:, :], start=True, stop=True).then_inc(S["any_turned"], 1)
                pe.wait_ge(S["any_z"], t + 1)
                pe.transpose(scan_ps[0:G, 0:P], z_one, ident[:, :]).then_inc(S["any_zt"], 1)
                pe.wait_ge(S["any_spread"], t + 1)
                for b in range(2):
                    last = pe.matmul(agg_ps[b][:, :], ones8[:, :], z_wide[:, b * HEADS:(b + 1) * HEADS, :],
                                     start=True, stop=True)
                last.then_inc(S["any_logits"], 1)
                pe.wait_ge(S["any_msg"], t + 1)
                pe.matmul(wt_ps[:, 0:G * GC], peers, msg_one.rearrange("p g k -> p (g k)"), start=True, stop=True
                          ).then_inc(S["any_agg"], 1)

            pe.wait_ge(S["order_known"], 1)
            with pe.If(pe.value_load(any_order[0:1, 0:1], min_val=0, max_val=1) > 0):
                with pe.Fori(0, tiles) as t:
                    any_tile(t)

        @block.scalar
        def _(act):
            for k, a in enumerate((a_src, a_dst, a_edge)):
                act.dma_start(a_in[:, k:k + 1], a.rearrange("h (d o) -> (h d) o", o=1)).then_inc(S["attn_in"], 16)
            def node_std(g, i, q):
                act.wait_ge(S["var_ready"], g + 1)
                act.activation(spread[:, q, 1, :], spread[:, q, 0, :], ACT.Sqrt).then_inc(S["std_ready"], 1)

            node_std(0, 0, 0)
            act.wait_ge(S["w_turned"], 1)
            act.activation(w_node[:, 0:P], agg_ps[0][:, 0:P], ACT.Copy)
            act.activation(w_node[:, NROW:NROW + P], agg_ps[0][:, P:2 * P], ACT.Copy)
            act.activation(w_edge_t[:, 0:P], agg_ps[0][:, 2 * P:3 * P], ACT.Copy)
            act.activation(w_node[:, P:NROW], agg_ps[1][:, 0:2 * HEADS], ACT.Copy)
            act.activation(w_edge_t[:, P:ROW], agg_ps[1][:, 2 * HEADS:3 * HEADS], ACT.Copy).then_inc(S["w_ready"], 1)

            def node_group(g, i, q):
                for j in range(NGRP):
                    n = g * NGRP + j
                    b = (q * NGRP + j) % 2
                    act.wait_ge(S["n_turned"], n + 1)
                    wait(act, S["n_proj"], n - 1)
                    act.activation(ht[:, b, :], turn_ps[b][:, 0:P], ACT.Relu).then_inc(S["ht_ready"], 1)
                    if j == NGRP // 2 and not (isinstance(g, int) and g == groups - 1):
                        node_std(g + 1, i, 1 - q)
                    if not (isinstance(g, int) and g == 0 and j == 0):
                        if j == 1:
                            wait(act, S["base_added"], g - 1)
                        node_row(n - 1, 1 - b, *((q, j - 1) if j else (1 - q, NGRP - 1)))

            def node_row(n, b, q, j):
                act.wait_ge(S["n_proj"], n + 1)
                act.activation(rows_out[:, bass.ds(n, 1), :].rearrange("p a f -> p (a f)"), proj_ps[b][:, 0:NROW],
                               ACT.Copy)
                act.activation(h_dst[:, q, j, :], proj_ps[b][:, NROW:2 * ROW], ACT.Copy).then_inc(S["node_rows"], 1)

            over(act, groups, 2, node_group)
            node_row(node_tiles - 1, (node_tiles - 1) % 2, (groups - 1) % 2, NGRP - 1)

            def turned_copy(c, i, q, m):
                act.wait_ge(S["turned_ready"], c * quads + m + 1)
                wait(act, S["proj_ready"], c * len(packs))
                act.activation(turned[:, 4 * m:4 * m + 4, :], turn_ps[m % 2][:, :].rearrange("p (a f) -> p a f", a=4),
                               ACT.Copy).then_inc(S["turned_out"], 1)

            def he_copy(c, i, q, n):
                if n == 0:
                    wait(act, S["msg_ready"], 2 * (c - BUFS + 1))
                act.wait_ge(S["proj_ready"], c * len(packs) + n + 1)
                act.activation(he[:, q, packs[n][0]:packs[n][-1] + 1, :],
                               proj_ps[n % 2][:, 0:len(packs[n]) * HROW].rearrange("p (a f) -> p a f", f=HROW), ACT.Copy
                               ).then_inc(S["he_ready"], 1)

            def front_rest(c, i, q):
                for n in range(len(packs)):
                    he_copy(c, i, q, n)
                    if n + 2 < quads:
                        turned_copy(c, i, q, n + 2)

            def exps(d):
                act.wait_ge(S["drop_ready"], d + 1)
                wait(act, S["diag_ready"], d)
                act.activation(rescale[:, :], drop[:, :], ACT.Exp).then_inc(S["rescale_ready"], 1)
                act.wait_ge(S["shifted_ready"], d + 1)
                wait(act, S["wt_ready"], d)
                act.activation(weights_t[:, :], shifted[:, :], ACT.Exp).then_inc(S["weights_ready"], 1)

            def put_weights(d, s):
                act.wait_ge(S["wt_ready"], d + 1)
                wait(act, S["agg_done"], 2 * d - 1 + s)
                a, b = s * HALF, (s + 1) * HALF
                act.activation(msg[:, a:b, :, DH:GC].rearrange("p t g o -> p (t g) o"),
                               wt_ps[:, a * G:b * G].rearrange("p (a o) -> p a o", o=1), ACT.Copy
                               ).then_inc(S["msg_den"], 1)

            def window_out(d, s):
                u = 2 * d + s
                act.wait_ge(S["agg_done"], u + 1)
                wait(act, S["result_ready"], d)
                act.activation(agg_sb[:, s, :], agg_ps[s][:, 0:G * GC], ACT.Copy).then_inc(S["agg_out"], 1)

            def step(c, i, q):
                after = ahead(c, i, q, 1)
                if after:
                    turned_copy(*after, 0)
                    turned_copy(*after, 1)
                exps(c)
                for s in range(2):
                    if not (isinstance(c, int) and c == 0):
                        window_out(c - 1, s)
                    put_weights(c, s)
                if after:
                    front_rest(*after)

            act.wait_ge(S["base_added"], groups)
            turned_copy(0, 0, 0, 0)
            turned_copy(0, 0, 0, 1)
            front_rest(0, 0, 0)
            over(act, chunks, BUFS, step)
            for s in range(2):
                window_out(chunks - 1, s)

            def any_tile(t):
                act.wait_ge(S["any_below"], t + 1)
                act.activation(below[:, :, :], below[:, :, :], ACT.Exp).then_inc(S["any_exps"], 1)

            act.wait_ge(S["order_known"], 1)
            with act.If(act.value_load(any_order[0:1, 0:1], min_val=0, max_val=1) > 0):
                with act.Fori(0, tiles) as t:
                    any_tile(t)

        @block.vector
        def _(v):
            v.memset(zeros[:, :], 0.0).then_inc(S["zero_done"], 1)
            v.memset(edst_parts[:, node_tiles, :, :], 0.0).then_inc(S["zero_done"], 1)
            v.memset(carry_hot[:, :, :], 0.0).then_inc(S["consts_done"], 1)
            v.memset(agg_sb[:, 1, :], 0.0).then_inc(S["consts_done"], 1)
            v.memset(ones8[:, :], 1.0).then_inc(S["consts_done"], 1)
            v.memset(across[:, :], -BIG).then_inc(S["consts_done"], 1)
            v.memset(no_peak[:, :], -BIG).then_inc(S["consts_done"], 1)
            v.memset(head_mask[:, :], 0.0).then_inc(S["w_step"], 1)
            v.wait_ge(S["w_step"], 1)
            for h in range(HEADS):
                last = v.memset(head_mask[h * DH:(h + 1) * DH, h:h + 1], 1.0)
            last.then_inc(S["w_step"], 1)
            def node_stats(g, i, q):
                wait(v, S["std_ready"], g - 1)
                for j in range(NGRP):
                    v.bn_stats(bn[:, q, j, :], xn[:, bass.ds(g * NGRP + j, 1), :].rearrange("p a f -> p (a f)")
                               ).then_inc(S["node_bn"], 1)
                for j in range(NGRP):
                    v.wait_ge(S["node_bn"], g * NGRP + j + 1)
                    v.bn_aggr(moments[:, q, j, :], bn[:, q, j, :]).then_inc(S["node_mv"], 1)
                v.wait_ge(S["node_mv"], (g + 1) * NGRP)
                v.tensor_scalar(spread[:, q, 0, :], moments[:, q, :, 1], EPS, None, ALU.add).then_inc(S["var_ready"], 1)

            v.wait_ge(S["x_first"], 16)
            node_stats(0, 0, 0)
            v.wait_ge(S["w_step"], 2)
            v.wait_ge(S["attn_in"], 48)
            v.tensor_tensor(a_diag[:, :, :], bc(head_mask[:, :], 1, 3), bc(a_in[:, :], 2, HEADS), ALU.mult
                            ).then_inc(S["w_step"], 1)
            v.wait_ge(S["iota_done"], 2)
            v.tensor_copy(iota_row[:, :], iota_i[:, :]).then_inc(S["consts_done"], 1)
            v.tensor_copy(iota_col[:, :], iota_ci[:, :]).then_inc(S["consts_done"], 1)
            v.wait_ge(S["ident_done"], 1)
            v.tensor_reduce(tile_mask[:, :], ident[:, :].rearrange("p (t g) -> p t g", g=G), AX.X, ALU.add
                            ).then_inc(S["consts_done"], 1)
            v.tensor_reduce(group_sel[:, :], ident[:, :].rearrange("p (t g) -> p g t", g=G), AX.X, ALU.add
                            ).then_inc(S["consts_done"], 1)
            v.tensor_copy(group_sel_t[:, :].rearrange("c (t g) -> c t g", g=G), bc(ident[0:G, 0:G], 1, TILES)
                          ).then_inc(S["consts_done"], 1)

            def node_group(g, i, q):
                v.wait_ge(S["std_ready"], g + 1)
                v.reciprocal(spread[:, q, 2, :], spread[:, q, 1, :]).then_inc(S["inv_ready"], 1)
                v.wait_ge(S["inv_ready"], g + 1)
                wait(v, S["n_turned"], (g - 1) * NGRP)
                for j in range(NGRP):
                    last = v.tensor_scalar(normal[:, q, j, :],
                                           xn[:, bass.ds(g * NGRP + j, 1), :].rearrange("p a f -> p (a f)"),
                                           moments[:, q, j, 0:1], spread[:, q, 2, j:j + 1], ALU.subtract, ALU.mult)
                last.then_inc(S["normed_ready"], 1)
                if isinstance(g, int) and g < 2:
                    v.wait_ge(S["x_rest" if g else "x_second"], 16)
                if not (isinstance(g, int) and g == groups - 1):
                    node_stats(g + 1, i, 1 - q)

            over(v, groups, 2, node_group)

            v.wait_ge(S["marks_in"], 16 * 9)
            v.tensor_tensor(rel[:, :].rearrange("p (u t) -> p u t", t=HALF),
                            dst_sb[:, :].rearrange("p (u t) -> p u t", t=HALF),
                            bc(hm_i[:, 0, :], 2, HALF), ALU.subtract).then_inc(S["marks_ready"], 1)
            v.wait_ge(S["consts_done"], 10)
            v.scalar_tensor_tensor(out=carry_sel[:, :], in0=hm_i[:, 2, :], scalar=iota_col[:, 0:1], in1=hm_i[:, 0, :],
                                   op0=ALU.add, op1=ALU.is_equal).then_inc(S["marks_ready"], 1)
            v.tensor_tensor(tile_keep[:, :, :], tm_i[:, :, :], tm_j[:, :, :], ALU.is_equal).then_inc(S["marks_ready"], 1)
            v.tensor_tensor(goes_on[:, :], hm_i[:, 1, :], hm_i[:, 0, :], ALU.is_equal).then_inc(S["marks_ready"], 1)
            v.wait_ge(S["marks_ready"], 4)
            v.tensor_tensor(carry_sel[:, :], carry_sel[:, :], goes_on[:, :], ALU.mult).then_inc(S["marks_ready"], 1)
            v.tensor_scalar(tile_keep[:, :, :], tile_keep[:, :, :], -0.5, 2 * BIG, ALU.add, ALU.mult
                            ).then_inc(S["marks_ready"], 1)
            v.wait_ge(S["marks_ready"], 6)
            v.tensor_tensor(line_steps, line[:, 1:tiles + 1], line[:, 0:tiles], ALU.subtract).then_inc(S["line_step"], 1)
            v.tensor_reduce(extremes[:, 1:2], rel[:, :], AX.X, ALU.min).then_inc(S["line_step"], 1)
            v.tensor_reduce(extremes[:, 2:3], rel[:, :], AX.X, ALU.max).then_inc(S["line_step"], 1)
            v.wait_ge(S["line_step"], 3)
            v.tensor_reduce(extremes[:, 0:1], line_steps, AX.X, ALU.min).then_inc(S["line_step"], 1)
            v.wait_ge(S["line_step"], 4)
            v.tensor_tensor(extremes[:, 0:1], extremes[:, 0:1], extremes[:, 1:2], ALU.min).then_inc(S["line_step"], 1)
            v.wait_ge(S["line_step"], 5)
            v.tensor_scalar(extremes[:, 0:1], extremes[:, 0:1], 0.0, None, ALU.is_lt).then_inc(S["line_step"], 1)
            v.tensor_scalar(extremes[:, 2:3], extremes[:, 2:3], float(P - 1), None, ALU.is_gt).then_inc(S["line_step"], 1)
            v.wait_ge(S["line_step"], 7)
            v.tensor_tensor(unfit[:, :], extremes[:, 0:1], extremes[:, 2:3], ALU.max).then_inc(S["unfit_ready"], 1)
            v.wait_ge(S["order_turned"], 1)
            v.tensor_reduce(any_order[:, :], wt_ps[0:1, 0:P], AX.X, ALU.max).then_inc(S["order_known"], 1)

            def one_hot(c, i, q, s):
                wait(v, S["agg_done"], 2 * (c - BUFS) + s + 1)
                v.tensor_tensor(hot[:, q, s * HALF:(s + 1) * HALF, :], bc(iota_row[:, :], 1, HALF),
                                bc(rel[:, bass.ds((2 * c + s) * HALF, HALF)], 2, P), ALU.is_equal
                                ).then_inc(S["hot_ready"], 1)

            def run_marks(c, i, q):
                v.wait_ge(runs_in[q], 16 * (i + 1))
                v.tensor_tensor(same[:, :, :], bc(runs[:, q, 0, :], 1, 2), runs[:, q, 1:3, :], ALU.is_equal
                                ).then_inc(S["same_ready"], 1)
                v.wait_ge(S["same_ready"], c + 1)
                v.tensor_scalar(keep[:, :, :], same[:, :, :], -0.5, 2 * BIG, ALU.add, ALU.mult
                                ).then_inc(S["keep_ready"], 1)

            def divide(d):
                def link(ins, step):
                    ins.then_inc(S["final_link"], 1)
                    v.wait_ge(S["final_link"], 3 * d + step)

                v.wait_ge(S["agg_out"], 2 * d + 2)
                window_sums = agg_sb[:, :, :].rearrange("p s (g k) -> p s g k", k=GC)
                link(v.tensor_scalar(divisors[:, :, :], window_sums[:, :, :, DH], 0.5, None, ALU.max), 1)
                link(v.reciprocal(divisors[:, :, :], divisors[:, :, :]), 2)
                link(v.tensor_tensor(shares[:, :, :, :].rearrange("p s g k -> p (s g) k"),
                                     agg_sb[:, :, :].rearrange("p s (g k) -> p (s g) k", k=GC)[:, :, 0:DH],
                                     bc(divisors[:, :, :].rearrange("p s g -> p (s g)"), 2, DH), ALU.mult), 3)

            def finish(d, i, q):
                wait(v, S["windows_out"], 32 * d)
                v.wait_ge(base_in[q], 32 * (i + 1))
                branches = shares[:, :, :, :].rearrange("p s (b h) k -> p s b (h k)", b=2)
                v.tensor_tensor(result[:, :, :], base_rows[:, q, :, :], branches[:, :, 0, :], ALU.add
                                ).then_inc(S["half_result"], 1)
                v.wait_ge(S["half_result"], d + 1)
                v.tensor_tensor(result[:, :, :], result[:, :, :], branches[:, :, 1, :], ALU.add
                                ).then_inc(S["result_ready"], 1)

            links = 9

            def softmax(d, i, q):
                done = [0]
                windows_before = not (isinstance(d, int) and d < 2)

                def link(ins):
                    done[0] += 1
                    ins.then_inc(S["chain"], 1)
                    v.wait_ge(S["chain"], d * links + done[0])

                for t in range(TILES):
                    v.wait_ge(gather_sem[t], 16 * (d + 1))
                v.wait_ge(S["he_ready"], (d + 1) * len(packs))
                link(v.tensor_reduce(edst_edge[:, :, :], he[:, q, :, ROW:HROW].rearrange("p t (a h) -> p t h a", a=PARTS),
                                     AX.X, ALU.add))
                wait(v, S["zt_ready"], d)
                v.tensor_tensor(z[:, :, 0:HEADS], rows[:, q, :, P:ROW], edst_edge[:, :, :], ALU.add)
                link(v.tensor_tensor(z[:, :, HEADS:G], he[:, q, :, P:ROW], edst_edge[:, :, :], ALU.add))
                v.scalar_tensor_tensor(out=z[:, :, :], in0=z[:, :, :], scalar=SLOPE, in1=z[:, :, :],
                                       op0=ALU.mult, op1=ALU.max).then_inc(S["z_ready"], 1)
                v.wait_ge(S["zt_ready"], d + 1)
                v.wait_ge(S["keep_ready"], d + 1)
                logits = scan_ps[:, 0:P]
                link(v.tensor_tensor_scan(run_fwd[:, :], keep[:, 0, :], logits, -BIG, ALU.min, ALU.max))
                link(v.tensor_tensor_scan(run_max[:, ::-1], keep[:, 1, ::-1], run_fwd[:, ::-1], -BIG, ALU.min, ALU.max))
                v.tensor_scalar(ends[:, 0, :], tile_mask[:, :], run_fwd[:, P - 1:P], None, ALU.mult)
                v.tensor_scalar(ends[:, 1, :], tile_mask[:, :], run_max[:, 0:1], None, ALU.mult
                                ).then_inc(S["ends_ready"], 1)
                W = TILES + 2
                wait(v, S["start_ready"], d)
                link(v.tensor_copy(across[:, 0:1], across[:, TILES:TILES + 1]))
                if windows_before:
                    divide(d - 2)
                v.wait_ge(S["across_in"], d + 1)
                v.tensor_tensor_scan(across[:, 1:TILES + 1], tile_keep[:, 0, bass.ds(d * TILES, TILES)],
                                     scan_ps[0:G, P:P + TILES], across[:, 0:1], ALU.min, ALU.max)
                v.tensor_tensor_scan(across[:, W - 1:W - 1 + TILES][:, ::-1],
                                     tile_keep[:, 1, bass.ds(d * TILES, TILES)],
                                     scan_ps[0:G, P + TILES:P + 2 * TILES][:, ::-1], -BIG, ALU.min, ALU.max
                                     ).then_inc(S["across_ready"], 1)
                if windows_before:
                    finish(d - 2, i + (q - 2) // BUFS, (q - 2) % BUFS)
                v.wait_ge(S["start_ready"], d + 1)
                link(v.tensor_tensor(start[:, :, :],
                                     scan_ps[:, P + 2 * TILES:P + 4 * TILES].rearrange("p (a t) -> p a t", a=2),
                                     bc(tile_mask[:, :], 1, 2), ALU.mult))
                link(v.tensor_reduce(init[:, :], start[:, :, :], AX.X, ALU.add))
                link(v.tensor_tensor_scan(run_fwd[:, :], keep[:, 0, :], logits, init[:, 0:1], ALU.min, ALU.max))
                link(v.tensor_tensor_scan(run_max[:, ::-1], keep[:, 1, ::-1], run_fwd[:, ::-1], init[:, 1:2],
                                          ALU.min, ALU.max))
                wait(v, S["rescale_ready"], d)
                v.tensor_scalar(drop[:, :], across[:, 0:1], run_max[0:G, 0:1], 0.0, ALU.subtract, ALU.min
                                ).then_inc(S["drop_ready"], 1)
                wait(v, S["weights_ready"], d)
                v.tensor_tensor(shifted[:, :], logits, run_max[:, :], ALU.subtract).then_inc(S["shifted_ready"], 1)
                v.wait_ge(S["rescale_ready"], d + 1)
                wait(v, S["factors_ready"], d)
                v.tensor_scalar(rescale_diag[:, :], ident[0:G, 0:G], rescale[:, 0:1], None, ALU.mult
                                ).then_inc(S["diag_ready"], 1)
                if ahead(d, i, q, 1):
                    run_marks(*ahead(d, i, q, 1))
                for s in range(2):
                    if s == 1 and ahead(d, i, q, 2):
                        one_hot(*ahead(d, i, q, 2), 0)
                    v.wait_ge(S["msg_den"], 2 * d + s + 1)
                    a, b = s * HALF, (s + 1) * HALF
                    w = msg[:, a:b, :, DH:GC]
                    v.tensor_tensor(msg[:, a:b, 0:HEADS, 0:DH],
                                    rows[:, q, a:b, 0:P].rearrange("p t (h k) -> p t h k", k=DH),
                                    w[:, :, 0:HEADS, :].to_broadcast([P, HALF, HEADS, DH]), ALU.mult)
                    v.tensor_tensor(msg[:, a:b, HEADS:G, 0:DH],
                                    he[:, q, a:b, 0:P].rearrange("p t (h k) -> p t h k", k=DH),
                                    w[:, :, HEADS:G, :].to_broadcast([P, HALF, HEADS, DH]), ALU.mult
                                    ).then_inc(S["msg_ready"], 1)
                wait(v, S["agg_done"], 2 * d)
                wait(v, S["agg_out"], 2 * d)
                v.tensor_copy(carry_hot[:, :, 0], carry_sel[:, bass.ds(2 * d, 2)])
                v.wait_ge(S["factors_ready"], d + 1)
                v.tensor_tensor(carry_in[:, :, :], agg_sb[:, 1, :].rearrange("p (g k) -> p g k", k=GC),
                                bc(scan_ps[:, P + 4 * TILES:P + 4 * TILES + G], 2, GC), ALU.mult
                                ).then_inc(S["carried"], 1)
                assert done[0] == links, done[0]

            def step(c, i, q):
                softmax(c, i, q)
                if ahead(c, i, q, 2):
                    one_hot(*ahead(c, i, q, 2), 1)

            v.wait_ge(S["table_out"], 16 * groups)
            v.wait_ge(S["split_ready"], groups)
            for c in range(2):
                for s in range(2):
                    one_hot(c, 0, c, s)
            run_marks(0, 0, 0)
            over(v, chunks, BUFS, step)
            for d in (chunks - 2, chunks - 1):
                divide(d)
                finish(d, d // BUFS, d % BUFS)

            any_links = 6

            def any_tile(t):
                done = [0]

                def link(ins):
                    done[0] += 1
                    ins.then_inc(S["any_step"], 1)
                    v.wait_ge(S["any_step"], t * any_links + done[0])

                v.wait_ge(S["any_in"], 16 * (t + 1))
                v.tensor_copy(src_one, src_all[:, bass.ds(t, 1)])
                v.tensor_copy(dst_one, dst_sb[:, bass.ds(t, 1)]).then_inc(S["any_ids"], 1)
                v.tensor_copy(dst_f[:, :], dst_sb[:, bass.ds(t, 1)]).then_inc(S["any_ids"], 1)
                v.wait_ge(S["any_fetched"], 64 * (t + 1))
                v.tensor_reduce(edst_edge[:, 0, :], edst_one.rearrange("p (a h) -> p h a", a=PARTS), AX.X, ALU.add)
                v.wait_ge(S["any_turned"], t + 1)
                link(v.tensor_scalar(peers, turn_ps[0][:, 0:P], dst_f[:, 0:1], None, ALU.is_equal))
                v.tensor_scalar(cap, peers, -0.5, 2 * BIG, ALU.add, ALU.mult)
                v.tensor_tensor(z_one[:, 0:HEADS], rows_one[:, P:ROW], edst_edge[:, 0, :], ALU.add)
                link(v.tensor_tensor(z_one[:, HEADS:G], proj_ps[0][:, P:ROW], edst_edge[:, 0, :], ALU.add))
                v.scalar_tensor_tensor(out=z_one, in0=z_one, scalar=SLOPE, in1=z_one, op0=ALU.mult, op1=ALU.max
                                       ).then_inc(S["any_z"], 1)
                v.wait_ge(S["any_zt"], t + 1)
                v.tensor_tensor(z_wide, bc(scan_ps[0:G, 0:P], 1, G), bc(ident[0:G, 0:G], 2, P), ALU.mult
                                ).then_inc(S["any_spread"], 1)
                v.wait_ge(S["any_logits"], t + 1)
                for b in range(2):
                    last = v.tensor_tensor(capped[:, b * HEADS:(b + 1) * HEADS, :],
                                           agg_ps[b][:, :].rearrange("p (g e) -> p g e", g=HEADS), bc(cap, 1, HEADS),
                                           ALU.min)
                link(last)
                link(v.tensor_reduce(peak_new[:, :], capped, AX.X, ALU.max))
                link(v.tensor_tensor(peak_new[:, :], peak_new[:, :], peak_old[:, :], ALU.max))
                v.tensor_tensor(below[:, 0, :], peak_old[:, :], peak_new[:, :], ALU.subtract)
                v.tensor_tensor(below[:, 1, :], z_one, peak_new[:, :], ALU.subtract).then_inc(S["any_below"], 1)
                v.wait_ge(S["any_exps"], t + 1)
                v.tensor_copy(msg_one[:, :, DH], below[:, 1, :])
                v.tensor_tensor(msg_one[:, 0:HEADS, 0:DH], rows_one[:, 0:P].rearrange("p (h k) -> p h k", k=DH),
                                bc(below[:, 1, 0:HEADS], 2, DH), ALU.mult)
                v.tensor_tensor(msg_one[:, HEADS:G, 0:DH], proj_ps[0][:, 0:P].rearrange("p (h k) -> p h k", k=DH),
                                bc(below[:, 1, HEADS:G], 2, DH), ALU.mult).then_inc(S["any_msg"], 1)
                link(v.tensor_tensor(sums_old.rearrange("p (g k) -> p g k", k=GC),
                                     sums_old.rearrange("p (g k) -> p g k", k=GC), bc(below[:, 0, :], 2, GC), ALU.mult))
                v.wait_ge(S["any_agg"], t + 1)
                v.tensor_tensor(sums_new, sums_old, wt_ps[:, 0:G * GC], ALU.add).then_inc(S["any_new"], 1)
                assert done[0] == any_links, done[0]

            def last_group(g):
                v.wait_ge(S[f"read_back{g % 2}"], 16 * (g // 2 + 1))
                v.tensor_scalar(inv[:, :, :], back[:, g % 2, :, :, DH], 0.5, None, ALU.max).then_inc(S["final_step"], 1)
                v.wait_ge(S["final_step"], 3 * g + 1)
                v.reciprocal(inv[:, :, :], inv[:, :, :]).then_inc(S["final_step"], 1)
                v.wait_ge(S["final_step"], 3 * g + 2)
                v.tensor_tensor(normed[:, :, :, :].rearrange("p t g k -> p (t g) k"),
                                back[:, g % 2, :, :, 0:DH].rearrange("p t g k -> p (t g) k"),
                                bc(inv[:, :, :].rearrange("p t g -> p (t g)"), 2, DH), ALU.mult).then_inc(S["final_step"], 1)
                v.wait_ge(S["final_step"], 3 * g + 3)
                rows_g = xn[:, g * NGRP:(g + 1) * NGRP, :]
                halves_n = normed[:, :, :, :].rearrange("p t (b h) k -> p t b (h k)", b=2)
                v.tensor_tensor(rows_g, rows_g, halves_n[:, :, 0, :], ALU.add).then_inc(S["sum_added"], 1)
                v.wait_ge(S["sum_added"], g + 1)
                v.tensor_tensor(rows_g, rows_g, halves_n[:, :, 1, :], ALU.add).then_inc(S["out_ready"], 1)


            with v.If(v.value_load(any_order[0:1, 0:1], min_val=0, max_val=1) > 0):
                with v.Fori(0, tiles) as t:
                    any_tile(t)
                for g in range(groups):
                    last_group(g)


def kernel(**inputs):
    import numpy as np
    import concourse.bacc as bacc
    from concourse.bass_utils import run_bass_kernel_spmd

    a = {k: np.asarray(v) for k, v in inputs.items()}
    n, e = a["x"].shape[0], a["src"].shape[0]
    node_rows = -(-n // (P * NGRP)) * P * NGRP
    chunks = -(-e // CHUNK)
    edges = chunks * CHUNK
    x = np.zeros((node_rows, P), np.float32)
    x[:n] = a["x"]
    src = np.zeros(edges, np.int32)
    src[:e] = a["src"]
    dst = np.full(edges + 2, n, np.int32)
    dst[0] = -1
    dst[1:e + 1] = a["dst"]
    dst[edges + 1] = -1
    here, before, after = dst[1:-1], dst[:-2], dst[2:]
    edge = np.zeros((edges, P), np.float32)
    edge[:e] = a["edge_attr_128"]
    edge = np.ascontiguousarray(edge.reshape(chunks, CHUNK, P).transpose(0, 2, 1))
    runs = np.stack([here, before, after], 0).reshape(3, chunks, TILES, 1, P)
    runs = np.ascontiguousarray(np.broadcast_to(runs, (3, chunks, TILES, G, P)).transpose(1, 2, 3, 0, 4))
    step = HALF * P
    first = here[::step]
    none = np.full(1, -1, np.int32)
    half_marks = np.stack([first, before[::step], np.concatenate([none, first[:-1]])])
    t_first, t_last = here[::P], here[P - 1::P]
    turn_back = lambda m: m.reshape(chunks, TILES)[:, ::-1].reshape(-1)
    tile_marks = np.stack([t_last, np.concatenate([none, t_last[:-1]]),
                           turn_back(t_first), turn_back(np.concatenate([t_first[1:], none]))])
    starts = (np.arange(P) * (edges // P))[:, None]
    dst_line = here[np.maximum(starts - 1 + np.arange(edges // P + 1)[None, :], 0)]
    arrays = {
        "x": x, "src_t": np.ascontiguousarray(src.reshape(-1, P).T), "dst_t": np.ascontiguousarray(here.reshape(-1, P).T),
        "dst_runs": runs.reshape(chunks, P, 3 * P), "half_marks": np.ascontiguousarray(half_marks),
        "tile_marks": np.ascontiguousarray(tile_marks), "dst_line": dst_line, "edge": edge,
        "w_src": a["L0_gnn_W_src"], "w_dst": a["L0_gnn_W_dst"], "w_edge": a["L0_gnn_W_edge"],
        "a_src": a["L0_gnn_attn_src"], "a_dst": a["L0_gnn_attn_dst"], "a_edge": a["L0_gnn_attn_edge"],
    }
    nc = bacc.Bacc("TRN2", target_bir_lowering=False, num_devices=1)
    aps = [nc.dram_tensor(k, v.shape, mybir.dt.from_np(v.dtype), kind="ExternalInput").ap() for k, v in arrays.items()]
    out = nc.dram_tensor("out", (node_rows + P, P), F32, kind="ExternalOutput").ap()
    gnn_program(nc, *aps, out, n)
    got = run_bass_kernel_spmd(nc, [arrays], core_ids=[0])
    return got.results[0]["out"][:n]
```
